# Optimizing a Trainium2 kernel written in Bass

```python
import numpy as np
import jax
import jax.numpy as jnp

def _softmax(x, axis=-1):
    return jax.nn.softmax(x, axis=axis)

def _gelu(x):
    return jax.nn.gelu(x, approximate=True)

def _silu(x):
    return jax.nn.silu(x)

def _sigmoid(x):
    return jax.nn.sigmoid(x)

def _layernorm(x, axis=-1, eps=1e-05):
    m = jnp.mean(x, axis=axis, keepdims=True)
    v = jnp.var(x, axis=axis, keepdims=True)
    return (x - m) / jnp.sqrt(v + eps)

def _scatter_add(tgt, idx, src, axis=0):
    return tgt.at[idx].add(src)

def _segment_sum(src, seg, n):
    return jax.ops.segment_sum(src, seg, n)
kernel_name = 'mk_seq_preln_d1_jaxref_r8_f7b0b5'

def setup_inputs(seed: int=0):
    np.random.seed(seed)
    _w = jnp.asarray

    def _L0_attn_setup():
        import jax, jax.numpy as jnp
        import numpy as np
        import math
        DIM, NHEAD, WINDOW = (128, 16, 128)
        DK = DIM // NHEAD
        key = jax.random.key(seed)
        k1, k2, k3 = jax.random.split(key, 3)
        x = jax.random.normal(k1, (4, 256, DIM), dtype=jnp.float32)
        w_qkv = jax.random.normal(k2, (3 * DIM, DIM), dtype=jnp.float32) * (1.0 / math.sqrt(DIM))
        w_proj = jax.random.normal(k3, (DIM, DIM), dtype=jnp.float32) * (1.0 / math.sqrt(DIM))
        return {'x': x, 'w_qkv': w_qkv, 'w_proj': w_proj}
    _L0_attn_in = _L0_attn_setup()

    def _L0_ffn_setup():
        import jax, jax.numpy as jnp
        import numpy as np
        TOPK = 8
        BN_EPS = 1e-05
        key = jax.random.key(seed)
        ks = jax.random.split(key, 5)
        b, n, d = (2, 128, 128)
        h, nk, kd = (8, 32, 128)
        ne = nk * nk
        scale = 0.02
        return {'inputs': jax.random.normal(ks[0], (b, n, d), jnp.float32), 'gamma': jnp.ones((d,), jnp.float32), 'beta': jnp.zeros((d,), jnp.float32), 'w_q': jax.random.normal(ks[1], (2 * h * kd, d), jnp.float32) * scale, 'keys': jax.random.normal(ks[2], (h, nk, 2, kd), jnp.float32) * scale, 'key_in': jax.random.normal(ks[3], (ne, d), jnp.float32) * scale, 'key_out': jax.random.normal(ks[4], (ne, d), jnp.float32) * scale}
    _L0_ffn_in = _L0_ffn_setup()
    _d = {'L0_attn_x': _L0_attn_in['x'], 'L0_attn_w_qkv': _L0_attn_in['w_qkv'], 'L0_attn_w_proj': _L0_attn_in['w_proj'], 'L0_ffn_gamma': _L0_ffn_in['gamma'], 'L0_ffn_beta': _L0_ffn_in['beta'], 'L0_ffn_w_q': _L0_ffn_in['w_q'], 'L0_ffn_keys': _L0_ffn_in['keys'], 'L0_ffn_key_in': _L0_ffn_in['key_in'], 'L0_ffn_key_out': _L0_ffn_in['key_out']}
    _x0 = _d['L0_attn_x']
    _d['L0_attn_x'] = jax.random.normal(jax.random.fold_in(jax.random.key(seed), 1), (16, 512, 128), dtype=_x0.dtype)
    del _x0
    return _d

def reference(L0_attn_x, L0_attn_w_qkv, L0_attn_w_proj, L0_ffn_gamma, L0_ffn_beta, L0_ffn_w_q, L0_ffn_keys, L0_ffn_key_in, L0_ffn_key_out):

    def _L0_attn_ref(x, w_qkv, w_proj):
        import jax, jax.numpy as jnp
        import numpy as np
        import math
        DIM, NHEAD, WINDOW = (128, 16, 128)
        DK = DIM // NHEAD
        B, T, C = x.shape
        qkv = jnp.einsum('btc,oc->bto', x, w_qkv)
        q, k, v = jnp.split(qkv, 3, axis=-1)

        def heads(t):
            return t.reshape(B, T, NHEAD, DK).transpose(0, 2, 1, 3)
        q, k, v = (heads(q), heads(k), heads(v))
        attn = jnp.einsum('bhqd,bhkd->bhqk', q, k) / math.sqrt(DK)
        idx = jnp.arange(T)
        mask = jnp.abs(idx[None, :] - idx[:, None]) > WINDOW
        attn = jnp.where(mask[None, None], -1000000000.0, attn)
        p = jax.nn.softmax(attn, axis=-1)
        out = jnp.einsum('bhqk,bhkd->bhqd', p, v)
        out = out.transpose(0, 2, 1, 3).reshape(B, T, C)
        return jnp.einsum('btc,oc->bto', out, w_proj)

    def _L0_ffn_ref(inputs, gamma, beta, w_q, keys, key_in, key_out):
        import jax, jax.numpy as jnp
        import numpy as np
        TOPK = 8
        BN_EPS = 1e-05
        b, n, d = inputs.shape
        h, nk, _, kd = keys.shape
        k = TOPK
        x = inputs.reshape(b * n, d)
        mu = jnp.mean(x, axis=0)
        var = jnp.mean(jnp.square(x - mu), axis=0)
        xn = (x - mu) * jax.lax.rsqrt(var + BN_EPS) * gamma + beta
        q = (xn @ w_q.T).reshape(b, n, 2, h, kd).transpose(2, 0, 1, 3, 4)
        sim = jnp.einsum('pbnhd,hkpd->pbnhk', q, keys)
        s, i = jax.lax.top_k(sim, k)
        sx, sy = (s[0], s[1])
        ix, iy = (i[0], i[1])
        all_scores = (sx[..., :, None] + sy[..., None, :]).reshape(b, n, h, k * k)
        all_idx = (ix[..., :, None] * nk + iy[..., None, :]).reshape(b, n, h, k * k)
        scores, pk = jax.lax.top_k(all_scores, k)
        idx = jnp.take_along_axis(all_idx, pk, axis=-1)
        w_down = key_in[idx]
        w_up = key_out[idx]
        o = jnp.einsum('bnd,bnhkd->bnhk', inputs, w_down)
        o = jax.nn.gelu(o, approximate=False) * jax.nn.softmax(scores, axis=-1)
        return jnp.einsum('bnhk,bnhkd->bnd', o, w_up)
    x = L0_attn_x
    x = x + _L0_attn_ref(_layernorm(x, axis=-1), L0_attn_w_qkv, L0_attn_w_proj)
    x = x + _L0_ffn_ref(_layernorm(x, axis=-1), L0_ffn_gamma, L0_ffn_beta, L0_ffn_w_q, L0_ffn_keys, L0_ffn_key_in, L0_ffn_key_out)
    return x

_drawn_inputs = setup_inputs


def setup_inputs(seed=0):
    import zlib

    import numpy as np

    out = dict(_drawn_inputs(seed))
    spreads = {'L0_ffn_gamma': (1.0, 0.6), 'L0_ffn_beta': (0.0, 0.8)}
    factors = {'L0_ffn_w_q': 8.0, 'L0_ffn_keys': 8.0, 'L0_ffn_key_in': 8.0, 'L0_ffn_key_out': 8.0}
    for name, (base, spread) in spreads.items():
        noise = np.random.default_rng([zlib.crc32(name.encode()), seed]).standard_normal(out[name].shape)
        drawn = base * np.exp(spread * noise) if base else spread * noise
        out[name] = jnp.asarray(drawn.astype(out[name].dtype))
    for name, factor in factors.items():
        out[name] = (out[name] * factor).astype(out[name].dtype)
    return out
```

```python
from contextlib import ExitStack

import concourse.bass as bass
from concourse import mybir

F32 = mybir.dt.float32
BF16 = mybir.dt.bfloat16
ACT = mybir.ActivationFunctionType
ALU = mybir.AluOpType
AX = mybir.AxisListType

P = 128
SEQS = 16
T = 512
TILES = T // P
H = 16
DK = P // H
EPS = 1e-5
TERMS = 9
KQ = TERMS * DK
SHIFT = 3
SLOT_V, SLOT_PT = 32, 1280


def attention(nc, ctx, x, w_qkvT, w_projT, identb, band, w_q, keysT, idf, bnst, KM, extra, x1_out, x2T_out):
    def sb(name, shape, dt=F32):
        return ctx.enter_context(nc.sbuf_tensor(name, shape, dt))

    def ps(name, shape, dt=F32):
        return ctx.enter_context(nc.psum_tensor(name, shape, dt))

    def sem(name):
        return ctx.enter_context(nc.semaphore(name))

    xs = x.rearrange("(s i p) c -> s p i c", i=TILES, p=P)
    x1s = x1_out.rearrange("(s i p) c -> s p i c", i=TILES, p=P)
    x2Ts = x2T_out.rearrange("c (s n) -> s c n", n=T)
    q_parts = nc.dram_tensor("q_parts", (3, P, T), BF16, kind="Internal").ap()
    k_parts = nc.dram_tensor("k_parts", (3, P, T), BF16, kind="Internal").ap()

    m_parts = nc.dram_tensor("m_parts", (3, H, T), BF16, kind="Internal").ap()

    wq = sb("wq", [P, 3 * P])
    wp = sb("wp", [P, P])
    WQF = sb("WQF", [P, 2 * FH, P])
    KT = sb("KT", [P, 2 * FH * NK])
    idb = sb("idb", [P, P], BF16)
    bandb = sb("bandb", [P, 2 * P], BF16)
    xin = [sb(f"xin{b}", [P, TILES, P]) for b in range(2)]
    xres = sb("xres", [P, TILES, P])
    st6 = sb("st6", [P, TILES, 6])
    mv = sb("mv", [P, TILES, 2])
    ve = sb("ve", [P, TILES])
    half = sb("half", [P, TILES])
    rs = sb("rs", [P, TILES])
    xn = sb("xn", [P, TILES, P])
    xnT = [sb(f"xnT{b}", [P, T]) for b in range(2)]
    qp = sb("qp", [P, 3, T], BF16)
    kp = sb("kp", [P, 3, T], BF16)
    rq = sb("rq", [P, T])
    rk = sb("rk", [P, T])
    Q = [sb(f"Q{b}", [P, H, T], BF16) for b in range(2)]
    K = [sb(f"K{b}", [P, H, T], BF16) for b in range(2)]
    V = [sb(f"V{b}", [P, TILES, H, SLOT_V]) for b in range(2)]
    mx = sb("mx", [P, H, TILES])
    mp = sb("mp", [H // 2, 3, T], BF16)
    rm = sb("rm", [H // 2, T])
    PT = sb("PT", [P, 8, SLOT_PT])
    U = [sb(f"U{b}", [P, 4, T]) for b in range(2)]
    rec = sb("rec", [P, TILES, H])
    A = sb("A", [P, TILES, P])
    AT = sb("AT", [P, T])
    X1 = sb("X1", [P, TILES, P])
    t6 = sb("t6", [P, TILES, 6])
    tv = sb("tv", [P, TILES, 2])
    te = sb("te", [P, TILES])
    trs = sb("trs", [P, TILES])
    X2 = sb("X2", [P, TILES, P])
    X2T = sb("X2T", [P, T])

    SX = ps("SX", [P, 2, 256])
    SY = ps("SY", [P, 2, 512])
    TX = ps("TX", [P, 2, 256])
    TY = ps("TY", [P, 2, 512])
    PV = ps("PV", [P, T])
    MB = ps("MB", [P, TILES, P])

    names = ("passed wrote_m memory km_p km_r consts ones ve_r rs_r xload xn_r xnT_p xnT_r q_p q1 q_r q2 q3 k_p k1 k_r k2 k3 v_p v_r "
             "wrote_q wrote_k back0 back1 sx sy sx_u sy_u tx ty tx_u ty_u masked pvm pv_u "
             "mt_p m1 m_r m2 m3 mrow att_p att_u at_p at_u pj_p x1_r te_r trs_r x2_r x2T_p x2T_r bn_r "
             "xres_l st_x1 st_x2 dv1 dv2 dv3 dv4 dv5 bn_all").split()
    S = {n: sem("a_" + n) for n in names}

    def steps(eng, do):
        for t in (-1, 0, 1):
            do(t, t)
        with eng.Fori(0, 6) as i:
            do(i * 2 + 2, 2)
            do(i * 2 + 3, 3)
        for t in (14, 15, 16, 17):
            do(t, t)

    def live(c, n):
        return 0 <= c < SEQS

    SHARED = [(1, "mt1", -1, "m_r", 2, 2), (3, "xnT", 1, "xnT_r", 1, 1), (4, "q", 1, "q_r", 1, 1),
              (5, "k", 1, "k_r", 1, 1), (6, "v", 0, "v_r", 1, 1),
              (7, "att0", -2, "att_u", 4, 1), (8, "att1", -2, "att_u", 4, 2), (9, "mt0", 0, "m_r", 2, 1),
              (10, "att2", -2, "att_u", 4, 3), (11, "att3", -2, "att_u", 4, 4), (12, "at", -2, "at_u", 1, 1),
              (13, "pj", -2, "x1_r", 1, 1), (15, "x2T", -2, "x2T_r", 1, 1)]
    ORDER = [n for _, n, *_ in SHARED]

    def bank_free(pe, name, t, c):
        at = ORDER.index(name)
        for back in range(1, len(SHARED) + 1):
            j, dt = (at - back) % len(SHARED), -1 if back > at else 0
            _, _, off, sname, per, nth = SHARED[j]
            if 0 <= c + dt + off < SEQS:
                pe.wait_ge(S[sname], (t + dt + off) * per + nth)
                return

    def await_(eng, semaphore, count):
        eng.wait_ge(semaphore, count)
        eng.sem_inc(S["passed"], 1)

    def one(ap, s):
        return ap[s]

    block = ctx.enter_context(nc.Block())

    @block.sync
    def _(sp):
        for dst, src in ((wq[:, :], w_qkvT), (wp[:, :], w_projT), (idb[:, :], identb), (bandb[:, :], band)):
            sp.dma_start(dst, src).then_inc(S["consts"], 16)
        for dst, src in extra[:1]:
            sp.dma_start(dst, src).then_inc(S["consts"], 16)
        for b in range(2):
            sp.dma_start(xin[b][:, :, :], xs[b]).then_inc(S["xload"], 16)
            sp.wait_ge(S["xload"], 16 * (b + 1))
        for dst, src in [(WQF[:, :, :], w_q.rearrange("(g k) d -> k g d", k=P)), (KT[:, :], keysT)] + extra[1:]:
            sp.dma_start(dst, src).then_inc(S["memory"], 16)

        def back(t, half_, b):
            hs = slice(8 * half_, 8 * half_ + 8)
            to = S["back0"] if half_ == 0 else S["back1"]
            for a in range(3):
                sp.dma_start(K[b][24 * a:24 * a + 24, hs, :],
                             k_parts.rearrange("a (d h) n -> (a d) h n", h=H)[:, hs, :]).then_inc(to, 16)
                for e in range(3):
                    r = 24 * a + 8 * e
                    sp.dma_start(Q[b][r:r + 8, hs, :],
                                 q_parts[a].rearrange("(d h) n -> d h n", h=H)[:, hs, :]).then_inc(to, 16)

        def shift_rows(t, half_, b):
            hs = slice(8 * half_, 8 * half_ + 8)
            sp.dma_start(m_parts[:, hs, :].rearrange("r h n -> h r n"), mp[:, :, :]).then_inc(S["wrote_m"], 16)
            await_(sp, S["wrote_m"], 16 * (2 * t + half_ + 1))
            sp.dma_start(Q[b][KQ:KQ + 3, hs, :], m_parts[:, hs, :]).then_inc(S["mrow"], 16)

        def step(t, c):
            if 0 <= c - 1 < SEQS:
                await_(sp, S["m3"], (t - 1) * 2 + 2)
                shift_rows(t - 1, 1, (c - 1) % 2)
            if 0 <= c + 1 < SEQS:
                await_(sp, S["q3"], t + 2)
                if c >= 0:
                    await_(sp, S["back0"], 16 * 12 * (t + 1))
                    await_(sp, S["back1"], 16 * 12 * (t + 1))
                sp.dma_start(q_parts.rearrange("a p n -> p a n"), qp[:, :, :]).then_inc(S["wrote_q"], 16)
                await_(sp, S["k3"], t + 2)
                sp.dma_start(k_parts.rearrange("a p n -> p a n"), kp[:, :, :]).then_inc(S["wrote_k"], 16)
                await_(sp, S["wrote_q"], 16 * (t + 2))
                await_(sp, S["wrote_k"], 16 * (t + 2))
                if c - 1 >= 0:
                    await_(sp, S["ty"], (t - 1) * H + 8)
                if c >= 0 and c + 2 < SEQS:
                    sp.dma_start(xin[c % 2][:, :, :], one(xs, t + 2)).then_inc(S["xload"], 16)
                back(t + 1, 0, (c + 1) % 2)
            if 0 <= c < SEQS:
                await_(sp, S["m3"], t * 2 + 1)
                shift_rows(t, 0, c % 2)
            if 0 <= c - 2 < SEQS:
                if c - 3 >= 0:
                    await_(sp, S["x1_r"], t - 2)
                sp.dma_start(xres[:, :, :], one(xs, t - 2)).then_inc(S["xres_l"], 16)
                await_(sp, S["x1_r"], t - 1)
                sp.dma_start(one(x1s, t - 2), X1[:, :, :]).then_inc(S["st_x1"], 16)
                await_(sp, S["x2T_r"], t - 1)
                sp.dma_start(one(x2Ts, t - 2), X2T[:, :]).then_inc(S["st_x2"], 16)
            if 0 <= c + 1 < SEQS:
                if c - 1 >= 0:
                    await_(sp, S["ty"], (t - 1) * H + 16)
                back(t + 1, 1, (c + 1) % 2)

        steps(sp, step)
        await_(sp, S["st_x1"], 16 * SEQS)
        await_(sp, S["st_x2"], 16 * SEQS)

    @block.gpsimd
    def _(pool):
        nc.gpsimd.memset(half[:, :], -0.5).then_inc(S["ones"], 1)
        for b in range(2):
            nc.gpsimd.memset(V[b][:, :, :, :], 0.0).then_inc(S["ones"], 1)
        pool.wait_ge(S["ones"], 3)
        nc.gpsimd.memset(K[0][64:P, :, :], 1.0).then_inc(S["ones"], 1)
        nc.gpsimd.memset(K[1][64:P, :, :], 1.0).then_inc(S["ones"], 1)
        pool.wait_ge(S["ones"], 5)
        for b in range(2):
            nc.gpsimd.memset(V[b][:, :, :, DK:DK + 1], 1.0).then_inc(S["ones"], 1)

        def mask(out, pairs, stop_low):
            s = 1 if stop_low else -1
            nc.gpsimd
            return nc.gpsimd.affine_select(out=out, in_=out, compare_op=ALU.is_ge, fill=0.0, base=0,
                                           pattern=([[0, 2]] if pairs else []) + [[s, P]], channel_multiplier=-s)

        def step(t, c):
            for h in range(H):
                if h == 2 and 0 <= c + 1 < SEQS:
                    pool.wait_ge(S["ve_r"], t + 2)
                    nc.gpsimd.tensor_tensor(rs[:, :], ve[:, :], half[:, :], ALU.pow).then_inc(S["rs_r"], 1)
                if 0 <= c - 1 < SEQS:
                    pt = PT[:, h % 8, :]
                    y = pt[:, 512:1280].rearrange("p (j n) -> p j n", j=2)
                    await_(pool, S["tx_u"], (t - 1) * H + h + 1)
                    mask(pt[:, 128:256], False, False).then_inc(S["masked"], 1)
                    mask(pt[:, 256:384], False, True).then_inc(S["masked"], 1)
                    await_(pool, S["ty_u"], (t - 1) * H + h + 1)
                    mask(y[:, :, 0:128], True, True).then_inc(S["masked"], 1)
                    mask(y[:, :, 256:384], True, False).then_inc(S["masked"], 1)
                if h == 14 and 0 <= c - 2 < SEQS:
                    pool.wait_ge(S["te_r"], t - 1)
                    nc.gpsimd.tensor_tensor(trs[:, :], te[:, :], half[:, :], ALU.pow).then_inc(S["trs_r"], 1)

        steps(pool, step)

    @block.scalar
    def _(act):
        act.wait_ge(S["ones"], 7)
        act.wait_ge(S["km_p"], 1)
        nc.scalar.copy(KM[:, :], MB[:, :, :].rearrange("p i n -> p (i n)")).then_inc(S["km_r"], 1)

        def step(t, c):
            b = c % 2
            for h in range(H):
                if h == 1 and 0 <= c - 1 < SEQS:
                    shift(t - 1, 2)
                if h == 9 and 0 <= c < SEQS:
                    shift(t, 1)
                if h == 3 and 0 <= c + 1 < SEQS:
                    act.wait_ge(S["xnT_p"], t + 2)
                    if c - 1 >= 0:
                        act.wait_ge(S["v_p"], t)
                    nc.scalar.copy(xnT[1 - b][:, :].rearrange("p (i n) -> p i n", n=P), MB[:, :, :]).then_inc(S["xnT_r"], 1)
                for hh, nm, src, dst, r, sc in ((4, "q", MB, qp, rq, DK ** -0.5), (5, "k", MB, kp, rk, 1.0)):
                    if h == hh and 0 <= c + 1 < SEQS:
                        act.wait_ge(S[nm + "_p"], t + 2)
                        if c >= 0:
                            act.wait_ge(S["wrote_" + nm], 16 * (t + 1))
                        nc.scalar.mul(dst[:, 0, :].rearrange("p (i n) -> p i n", n=P), src[:, :, :], sc).then_inc(S[nm + "1"], 1)
                    if h == hh + 1 and 0 <= c + 1 < SEQS:
                        act.wait_ge(S[nm + "_r"], t + 2)
                        nc.scalar.copy(dst[:, 1, :], r[:, :]).then_inc(S[nm + "2"], 1)
                if h == 6 and 0 <= c < SEQS:
                    act.wait_ge(S["v_p"], t + 1)
                    if c >= 2:
                        act.wait_ge(S["pvm"], (t - 1) * 4)
                    nc.scalar.copy(V[b][:, :, :, 0:DK], MB[:, :, :].rearrange("p i (h d) -> p i h d", d=DK)).then_inc(S["v_r"], 1)
                for g, (sl, ds_) in enumerate(((6, 1), (10, 1), (14, 1), (2, 2))):
                    if h == sl and 0 <= c - ds_ < SEQS:
                        act.wait_ge(S["pvm"], (t - ds_) * 4 + g + 1)
                        if c - ds_ >= 2:
                            act.wait_ge(S["att_p"], (t - ds_ - 1) * 4)
                        nc.scalar.copy(U[(c - ds_) % 2][:, g, :], PV[:, :]).then_inc(S["pv_u"], 1)
                if h == 12 and 0 <= c - 2 < SEQS:
                    act.wait_ge(S["at_p"], t - 1)
                    nc.scalar.copy(AT[:, :].rearrange("p (i n) -> p i n", n=P), MB[:, :, :]).then_inc(S["at_u"], 1)
                if h == 15 and 0 <= c - 2 < SEQS:
                    act.wait_ge(S["x2T_p"], t - 1)
                    if c - 2 >= 1:
                        act.wait_ge(S["st_x2"], 16 * (t - 2))
                        act.wait_ge(S["bn_r"], t - 2)
                    nc.scalar.copy(X2T[:, :].rearrange("p (i n) -> p i n", n=P), MB[:, :, :]).then_inc(S["x2T_r"], 1)
                if 0 <= c - 1 < SEQS:
                    pt = PT[:, h % 8, :]
                    n = (t - 1) * H + h + 1
                    act.wait_ge(S["tx"], n)
                    if h >= 8:
                        act.wait_ge(S["pvm"], (t - 1) * 4 + (h - 8) // 4 + 1)
                    elif c - 1 >= 1:
                        act.wait_ge(S["pvm"], (t - 2) * 4 + 2 + h // 4 + 1)
                    nc.scalar.activation(pt[:, 0:512], TX[:, :, :].rearrange("p j n -> p (j n)"), ACT.Exp).then_inc(S["tx_u"], 1)
                    act.wait_ge(S["ty"], n)
                    nc.scalar.activation(pt[:, 512:1280].rearrange("p (j n) -> p j n", j=2), TY[:, :, 0:384], ACT.Exp).then_inc(S["ty_u"], 1)

        def shift(s, nth):
            act.wait_ge(S["mt_p"], s * 2 + nth)
            prev = (s * 2 + nth - 1)
            if not isinstance(prev, int) or prev >= 1:
                act.wait_ge(S["mrow"], prev * 16)
            nc.scalar.mul(mp[:, 0, :].rearrange("p (i n) -> p i n", n=P), MB[0:8, :, :], -1.0).then_inc(S["m1"], 1)
            act.wait_ge(S["m_r"], s * 2 + nth)
            nc.scalar.copy(mp[:, 1, :], rm[:, :]).then_inc(S["m2"], 1)

        steps(act, step)

    @block.vector
    def _(dve):
        dve.wait_ge(S["consts"], 80)

        def stats(s, src, a6, av, ae, s1, s2, to):
            for i in range(TILES):
                nc.vector.bn_stats(a6[:, i, :], src[:, i, :]).then_inc(s1, 1)
            await_(dve, s1, (s + 1) * TILES)
            for i in range(TILES):
                nc.vector.bn_aggr(av[:, i, :], a6[:, i, :]).then_inc(s2, 1)
            dve.wait_ge(s2, (s + 1) * TILES)
            nc.vector.tensor_scalar(ae[:, :], av[:, :, 1], EPS, None, ALU.add).then_inc(to, 1)

        def norm(src, av, r, dst, to):
            for i in range(TILES):
                o = nc.vector.tensor_scalar(dst[:, i, :], src[:, i, :], av[:, i, 0:1], r[:, i:i + 1], ALU.subtract, ALU.mult)
            o.then_inc(to, 1)

        def shift(s, nth):
            dve.wait_ge(S["m1"], s * 2 + nth)
            nc.vector.scalar_tensor_tensor(out=rm[:, :].rearrange("p (i n) -> p i n", n=P), in0=MB[0:8, :, :], scalar=-1.0,
                                           in1=mp[:, 0, :].rearrange("p (i n) -> p i n", n=P), op0=ALU.mult, op1=ALU.subtract).then_inc(S["m_r"], 1)
            dve.wait_ge(S["m2"], s * 2 + nth)
            nc.vector.tensor_tensor(mp[:, 2, :], rm[:, :], mp[:, 1, :], ALU.subtract).then_inc(S["m3"], 1)

        def step(t, c):
            b = c % 2
            for h in range(H):
                if h == 1 and 0 <= c - 1 < SEQS:
                    shift(t - 1, 2)
                if h == 9 and 0 <= c < SEQS:
                    shift(t, 1)
                if h == 1 and 0 <= c + 1 < SEQS:
                    dve.wait_ge(S["xload"], 16 * (t + 2))
                    stats(t + 1, xin[1 - b], st6, mv, ve, S["dv1"], S["dv2"], S["ve_r"])
                if h == 3 and 0 <= c + 1 < SEQS:
                    dve.wait_ge(S["rs_r"], t + 2)
                    if c >= 0:
                        dve.wait_ge(S["xnT_p"], t + 1)
                    norm(xin[1 - b], mv, rs, xn, S["xn_r"])
                for hh, nm, dst, r, sc in ((4, "q", qp, rq, DK ** -0.5), (5, "k", kp, rk, 1.0)):
                    if h == hh and 0 <= c + 1 < SEQS:
                        dve.wait_ge(S[nm + "1"], t + 2)
                        nc.vector.scalar_tensor_tensor(out=r[:, :].rearrange("p (i n) -> p i n", n=P), in0=MB[:, :, :], scalar=sc,
                                                       in1=dst[:, 0, :].rearrange("p (i n) -> p i n", n=P),
                                                       op0=ALU.mult, op1=ALU.subtract).then_inc(S[nm + "_r"], 1)
                    if h == hh + 1 and 0 <= c + 1 < SEQS:
                        dve.wait_ge(S[nm + "2"], t + 2)
                        nc.vector.tensor_tensor(dst[:, 2, :], r[:, :], dst[:, 1, :], ALU.subtract).then_inc(S[nm + "3"], 1)
                for i, sl in enumerate((7, 8, 10, 11)):
                    if h == sl and 0 <= c - 2 < SEQS:
                        n = (t - 2) * 4 + i + 1
                        dve.wait_ge(S["att_p"], n)
                        hv = MB[:, :, :].rearrange("p g (h e) -> p (g h) e", e=SLOT_V)
                        nc.vector.reciprocal(rec[:, i, :], hv[:, :, DK]).then_inc(S["dv3"], 1)
                        dve.wait_ge(S["dv3"], n)
                        nc.vector.tensor_tensor(A[:, i, :].rearrange("p (h d) -> p h d", d=DK), hv[:, :, 0:DK],
                                                rec[:, i, :].unsqueeze(2).broadcast_to([P, H, DK]), ALU.mult).then_inc(S["att_u"], 1)
                if h == 13 and 0 <= c - 2 < SEQS:
                    dve.wait_ge(S["pj_p"], t - 1)
                    dve.wait_ge(S["xres_l"], 16 * (t - 1))
                    if c - 2 >= 1:
                        dve.wait_ge(S["st_x1"], 16 * (t - 2))
                    nc.vector.tensor_tensor(X1[:, :, :], MB[:, :, :], xres[:, :, :], ALU.add).then_inc(S["x1_r"], 1)
                    dve.wait_ge(S["x1_r"], t - 1)
                    stats(t - 2, X1, t6, tv, te, S["dv4"], S["dv5"], S["te_r"])
                if h == 15 and 0 <= c - 2 < SEQS:
                    dve.wait_ge(S["trs_r"], t - 1)
                    norm(X1, tv, trs, X2, S["x2_r"])
                if 0 <= c < SEQS:
                    n = t * H + h + 1
                    dve.wait_ge(S["sx"], n)
                    if h == 0 and c >= 1:
                        dve.wait_ge(S["mt_p"], t * 2 - 1)
                    if h == 8 and c >= 1:
                        dve.wait_ge(S["mt_p"], t * 2)
                    nc.vector.tensor_reduce(mx[:, h, 0:4:3], SX[:, :, :], AX.X, ALU.max).then_inc(S["sx_u"], 1)
                    dve.wait_ge(S["sy"], n)
                    nc.vector.tensor_reduce(mx[:, h, 1:3], SY[:, :, 0:384], AX.X, ALU.max).then_inc(S["sy_u"], 1)
            if 0 <= c - 2 < SEQS:
                dve.wait_ge(S["x2T_r"], t - 1)
                nc.vector.bn_stats(bnst[:, t - 2, :] if isinstance(t, int) else bnst[:, bass.ds(t - 2, 1), :].rearrange("p o n -> p (o n)"), X2T[:, :]).then_inc(S["bn_r"], 1)

        steps(dve, step)

    @block.tensor
    def _(pe):
        pe.wait_ge(S["consts"], 80)
        pe.wait_ge(S["ones"], 7)
        mb = MB[:, :, :].rearrange("p i n -> p (i n)")
        pe.wait_ge(S["memory"], 16 * (2 + len(extra) - 1))
        for g in range(2 * FH):
            o = pe.matmul(mb[:, g * NK:(g + 1) * NK], WQF[:, g, :], KT[:, g * NK:(g + 1) * NK], start=True, stop=True)
        o.then_inc(S["km_p"], 1)
        pe.wait_ge(S["km_r"], 1)
        LO, HI = bandb[:, 0:P], bandb[:, P:2 * P]

        def scores(t, c, h):
            b, n = c % 2, t * H + h + 1
            if h == 0:
                pe.wait_ge(S["back0"], 192 * (t + 1))
            if h == 8:
                pe.wait_ge(S["back1"], 192 * (t + 1))

            def tile(out, i, k0, k1):
                lo, hi = i > 0, i < TILES - 1
                pe.matmul(out[:, 0:(k1 - k0) * P], Q[b][0:KQ, h, i * P:(i + 1) * P], K[b][0:KQ, h, k0 * P:k1 * P],
                          start=True, stop=False, skip_group_check=True)
                if lo:
                    o = pe.matmul(out[:, 0:P], idb[:, :], LO, start=False, stop=not hi, skip_group_check=True)
                if hi:
                    o = pe.matmul(out[:, (k1 - k0 - 1) * P:(k1 - k0) * P], idb[:, :], HI, start=False, stop=True, skip_group_check=True)
                return o

            if c > 0 or h > 0:
                pe.wait_ge(S["sx_u"], n - 1)
            tile(SX[:, 0, :], 0, 0, 2)
            tile(SX[:, 1, :], 3, 2, 4).then_inc(S["sx"], 1)
            if c > 0 or h > 0:
                pe.wait_ge(S["sy_u"], n - 1)
            tile(SY[:, 0, :], 1, 0, 3)
            tile(SY[:, 1, :], 2, 1, 4).then_inc(S["sy"], 1)

        def scoresT(t, c, h):
            s = t - 1
            b, n = (c - 1) % 2, s * H + h + 1
            R = KQ + SHIFT
            if h == 0:
                pe.wait_ge(S["mrow"], 32 * s + 16)
            if h == 8:
                pe.wait_ge(S["mrow"], 32 * s + 32)

            def tile(out, j, q0, q1):
                return pe.matmul(out[:, 0:(q1 - q0) * P], K[b][0:R, h, j * P:(j + 1) * P], Q[b][0:R, h, q0 * P:q1 * P],
                                 start=True, stop=True, skip_group_check=True)

            if c > 1 or h > 0:
                pe.wait_ge(S["tx_u"], n - 1)
            tile(TX[:, 0, :], 0, 0, 2)
            tile(TX[:, 1, :], 3, 2, 4).then_inc(S["tx"], 1)
            if c > 1 or h > 0:
                pe.wait_ge(S["ty_u"], n - 1)
            tile(TY[:, 0, :], 1, 0, 3)
            tile(TY[:, 1, :], 2, 1, 4).then_inc(S["ty"], 1)

        SPAN = [(0, 0, 2), (512, 0, 3), (896, 1, 4), (256, 2, 4)]

        def values(s, c, g):
            b = c % 2
            pe.wait_ge(S["masked"], (s * H + 4 * g + 4) * 4)
            if g == 0:
                pe.wait_ge(S["v_r"], s + 1)
            if c > 0 or g > 0:
                pe.wait_ge(S["pv_u"], s * 4 + g)
            for j, (at, q0, q1) in enumerate(SPAN):
                for e in range(4):
                    h = 4 * g + e
                    o = pe.matmul(PV[32 * e:32 * e + 32, q0 * P:q1 * P], V[b][:, j, h, :],
                                  PT[:, h % 8, at:at + (q1 - q0) * P], start=(j == 0), stop=(j == 3), skip_group_check=True)
            o.then_inc(S["pvm"], 1)

        def step(t, c):
            b = c % 2
            for h in range(H):
                if h == 1 and 0 <= c - 1 < SEQS:
                    bank_free(pe, "mt1", t, c)
                    pe.wait_ge(S["sy_u"], t * H)
                    for i in range(TILES):
                        o = pe.transpose(MB[0:8, i, :], mx[:, 8:16, i], idf[:, :])
                    o.then_inc(S["mt_p"], 1)
                if h == 9 and 0 <= c < SEQS:
                    bank_free(pe, "mt0", t, c)
                    pe.wait_ge(S["sy_u"], t * H + 8)
                    for i in range(TILES):
                        o = pe.transpose(MB[0:8, i, :], mx[:, 0:8, i], idf[:, :])
                    o.then_inc(S["mt_p"], 1)
                if h == 3 and 0 <= c + 1 < SEQS:
                    bank_free(pe, "xnT", t, c)
                    pe.wait_ge(S["xn_r"], t + 2)
                    for i in range(TILES):
                        o = pe.transpose(MB[:, i, :], xn[:, i, :], idf[:, :])
                    o.then_inc(S["xnT_p"], 1)
                if h == 4 and 0 <= c + 1 < SEQS:
                    bank_free(pe, "q", t, c)
                    pe.wait_ge(S["xnT_r"], t + 2)
                    pe.matmul(MB[:, :, :], wq[:, 0:P], xnT[1 - b][:, :], start=True, stop=True).then_inc(S["q_p"], 1)
                if h == 5 and 0 <= c + 1 < SEQS:
                    bank_free(pe, "k", t, c)
                    pe.matmul(MB[:, :, :], wq[:, P:2 * P], xnT[1 - b][:, :], start=True, stop=True).then_inc(S["k_p"], 1)
                if h == 6 and 0 <= c < SEQS:
                    bank_free(pe, "v", t, c)
                    for i in range(TILES):
                        o = pe.matmul(MB[:, i, :], xnT[b][:, i * P:(i + 1) * P], wq[:, 2 * P:3 * P], start=True, stop=True)
                    o.then_inc(S["v_p"], 1)
                for i, sl in enumerate((7, 8, 10, 11)):
                    if h == sl and 0 <= c - 2 < SEQS:
                        bank_free(pe, f"att{i}", t, c)
                        pe.wait_ge(S["pv_u"], (t - 1) * 4)
                        for g in range(4):
                            o = pe.transpose(MB[:, g, :], U[b][:, g, i * P:(i + 1) * P], idf[:, :])
                        o.then_inc(S["att_p"], 1)
                if h == 12 and 0 <= c - 2 < SEQS:
                    bank_free(pe, "at", t, c)
                    for i in range(TILES):
                        o = pe.transpose(MB[:, i, :], A[:, i, :], idf[:, :])
                    o.then_inc(S["at_p"], 1)
                if h == 13 and 0 <= c - 2 < SEQS:
                    bank_free(pe, "pj", t, c)
                    for i in range(TILES):
                        o = pe.matmul(MB[:, i, :], AT[:, i * P:(i + 1) * P], wp[:, :], start=True, stop=True)
                    o.then_inc(S["pj_p"], 1)
                if h == 15 and 0 <= c - 2 < SEQS:
                    bank_free(pe, "x2T", t, c)
                    pe.wait_ge(S["x2_r"], t - 1)
                    for i in range(TILES):
                        o = pe.transpose(MB[:, i, :], X2[:, i, :], idf[:, :])
                    o.then_inc(S["x2T_p"], 1)
                for g, (sl, ds_) in enumerate(((6, 1), (10, 1), (14, 1), (2, 2))):
                    if h == sl and 0 <= c - ds_ < SEQS:
                        values(t - ds_, c - ds_, g)
                if 0 <= c < SEQS:
                    scores(t, c, h)
                if 0 <= c - 1 < SEQS:
                    scoresT(t, c, h)

        steps(pe, step)


GROUPS = 16
GT = 4
GN = GT * P
FH = 8
NK = 32
NE = NK * NK
BLK = NE // P
TOPK = 8
CAND = 20
VSUM = (4,)
RING = 4


def ffn(nc, ctx, x1, x2T, KM, key_in, key_out, gb, ident, bnst, out):
    def sb(name, shape, dt=F32):
        return ctx.enter_context(nc.sbuf_tensor(name, shape, dt))

    def ps(name, shape, dt=F32):
        return ctx.enter_context(nc.psum_tensor(name, shape, dt))

    def sem(name):
        return ctx.enter_context(nc.semaphore(name))

    x1g = x1.rearrange("(g i p) c -> g p i c", i=GT, p=P)
    outg = out.rearrange("(g i p) c -> g p i c", i=GT, p=P)
    x2Tg = x2T.rearrange("c (g n) -> g c n", n=GN)

    mvb = sb("mvb", [P, 2])
    vb = sb("vb", [P, 1])
    hb = sb("hb", [P, 1])
    rb = sb("rb", [P, 1])
    ab = sb("ab", [P, 2])
    X2T = [sb(f"X2T{b}", [P, GN]) for b in range(2)]
    X1 = [sb(f"X1{b}", [P, GT, P]) for b in range(2)]
    BNT = [sb(f"BNT{b}", [P, GN]) for b in range(2)]
    GE = [sb(f"GE{b}", [P, BLK, GN]) for b in range(2)]
    OUT = [sb(f"OUT{b}", [P, GT, P]) for b in range(2)]
    SIM = [sb(f"SIM{b}", [P, 2, FH, NK]) for b in range(4)]
    M8 = [sb(f"M8{b}", [P, 2, FH, TOPK]) for b in range(2)]
    CD = sb("CD", [P, FH, CAND])
    TOP = [sb(f"TOP{b}", [P, FH, TOPK]) for b in range(2)]
    D8 = sb("D8", [P, FH, TOPK])
    E8 = sb("E8", [P, FH, TOPK])
    Z = sb("Z", [P, FH])
    LZ = sb("LZ", [P, FH])
    NB = [sb(f"NB{b}", [P, FH]) for b in range(2)]
    SUM = [sb(f"SUM{b}", [P, NE]) for b in range(RING)]
    W = [sb(f"W{b}", [P, NE]) for b in range(RING)]
    CT = [sb(f"CT{b}", [P, BLK, P]) for b in range(2)]

    WT = [ps(f"WT{b}", [P, BLK, P]) for b in range(2)]
    PSIM = ps("PSIM", [P, 2 * FH * NK])
    PO = [ps(f"PO{b}", [P, GN]) for b in range(2)]
    POUT = ps("POUT", [P, 512])

    names = ("passed half stat var pow coef x1l x2l bnt sim_p sim psum vsum e masked turned ct outp outs o_p ge stored "
             "m8 cd top d8 e8 z lz nb").split()
    S = {n: sem("f_" + n) for n in names}

    def steps(eng, do):
        do(0, 0, True)
        do(1, 1, True)
        with eng.Fori(1, GROUPS // 2 - 1) as i:
            do(i * 2, 0, True)
            do(i * 2 + 1, 1, True)
        do(GROUPS - 2, 0, True)
        do(GROUPS - 1, 1, False)

    def first(g, b):
        return isinstance(g, int) and g == 0

    def wait_pos(eng, s, v):
        if not isinstance(v, int) or v > 0:
            eng.wait_ge(s, v)

    def await_(eng, semaphore, count):
        eng.wait_ge(semaphore, count)
        eng.sem_inc(S["passed"], 1)

    block = ctx.enter_context(nc.Block())

    @block.sync
    def _(sp):
        sp.dma_start(X2T[0][:, :], x2Tg[0]).then_inc(S["x2l"], 16)
        sp.dma_start(X1[0][:, :, :], x1g[0]).then_inc(S["x1l"], 16)

        def group(g, b, more):
            if more:
                await_(sp, S["x2l"], (g + 1) * 16)
                await_(sp, S["x1l"], (g + 1) * 16)
                await_(sp, S["outs"], g * GT)
                sp.dma_start(X2T[1 - b][:, :], x2Tg[g + 1]).then_inc(S["x2l"], 16)
                sp.dma_start(X1[1 - b][:, :, :], x1g[g + 1]).then_inc(S["x1l"], 16)
            await_(sp, S["outs"], (g + 1) * GT)
            sp.dma_start(outg[g], OUT[b][:, :, :]).then_inc(S["stored"], 16)
            await_(sp, S["stored"], (g + 1) * 16)

        steps(sp, group)

    def pair_sums(eng, j, h, q):
        sx = SIM[q][:, 0, h, :].unsqueeze(2).broadcast_to([P, NK, NK])
        sy = SIM[q][:, 1, h, :].unsqueeze(1).broadcast_to([P, NK, NK])
        return eng.tensor_tensor(SUM[h % RING][:, :].rearrange("p (i j) -> p i j", i=NK), sx, sy, ALU.add)

    def sum_buffer_free(eng, j, h):
        wait_pos(eng, S["masked"], j * FH + h - RING + 1)

    @block.gpsimd
    def _(pool):
        nc.gpsimd.memset(hb[:, :], -0.5).then_inc(S["half"], 1)
        pool.wait_ge(S["half"], 1)
        pool.wait_ge(S["var"], 1)
        nc.gpsimd.tensor_tensor(rb[:, :], vb[:, :], hb[:, :], ALU.pow).then_inc(S["pow"], 1)

        def group(g, b, more):
            for k in range(GT):
                j = g * GT + k
                pool.wait_ge(S["sim"], j + 1)
                for h in range(FH):
                    if h in VSUM:
                        continue
                    sum_buffer_free(pool, j, h)
                    pair_sums(nc.gpsimd, j, h, k).then_inc(S["psum"], 1)

        steps(pool, group)

    @block.scalar
    def _(act):
        def sim_copy(j, q):
            act.wait_ge(S["sim_p"], j + 1)
            nc.scalar.copy(SIM[q][:, :, :, :].rearrange("p a h k -> p (a h k)"), PSIM[:, :]).then_inc(S["sim"], 1)

        def gelus(g, b):
            for e in range(BLK):
                act.wait_ge(S["o_p"], g * BLK + e + 1)
                nc.scalar.activation(GE[b][:, e, :], PO[e % 2][:, :], ACT.Gelu).then_inc(S["ge"], 1)

        gelus(0, 0)
        sim_copy(0, 0)
        sim_copy(1, 1)

        def small_exp(j):
            act.wait_ge(S["d8"], j + 1)
            nc.scalar.activation(E8[:, :, :].rearrange("p h k -> p (h k)"), D8[:, :, :].rearrange("p h k -> p (h k)"), ACT.Exp).then_inc(S["e8"], 1)

        def small_ln(j):
            act.wait_ge(S["z"], j + 1)
            nc.scalar.activation(LZ[:, :], Z[:, :], ACT.Ln).then_inc(S["lz"], 1)

        small_exp(0)
        small_ln(0)

        def group(g, b, more):
            for k in range(GT):
                j = g * GT + k
                q = k % 2
                nxt = more or k < GT - 1
                for h in range(FH):
                    if h == 0:
                        act.wait_ge(S["nb"], j + 1)
                    if h == 2 and (more or k < 2):
                        wait_pos(act, S["psum"], (j - 1) * (FH - len(VSUM)))
                        wait_pos(act, S["vsum"], (j - 1) * len(VSUM))
                        sim_copy(j + 2, (k + 2) % 4)
                    if h == 0 and k == 2 and more:
                        gelus(g + 1, 1 - b)
                    if h in VSUM:
                        act.wait_ge(S["vsum"], j * len(VSUM) + VSUM.index(h) + 1)
                    else:
                        act.wait_ge(S["psum"], j * (FH - len(VSUM)) + sum(1 for e in range(h) if e not in VSUM) + 1)
                    wait_pos(act, S["turned"], j * FH + h - RING + 1)
                    nc.scalar.activation(W[h % RING][:, :], SUM[h % RING][:, :], ACT.Exp, bias=NB[q][:, h:h + 1]).then_inc(S["e"], 1)
                    if h == 5 and nxt:
                        small_exp(j + 1)
                    if h == 6 and nxt:
                        small_ln(j + 1)

        steps(act, group)

    @block.vector
    def _(dve):
        nc.vector.bn_aggr(mvb[:, :], bnst[:, :, :].rearrange("p s n -> p (s n)")).then_inc(S["stat"], 1)
        dve.wait_ge(S["stat"], 1)
        nc.vector.tensor_scalar(vb[:, :], mvb[:, 1:2], EPS, None, ALU.add).then_inc(S["var"], 1)
        dve.wait_ge(S["pow"], 1)
        nc.vector.tensor_tensor(ab[:, 0:1], rb[:, :], gb[:, 0:1], ALU.mult).then_inc(S["coef"], 1)
        dve.wait_ge(S["coef"], 1)
        nc.vector.tensor_tensor(mvb[:, 1:2], mvb[:, 0:1], ab[:, 0:1], ALU.mult).then_inc(S["coef"], 1)
        dve.wait_ge(S["coef"], 2)
        nc.vector.tensor_tensor(ab[:, 1:2], gb[:, 1:2], mvb[:, 1:2], ALU.subtract).then_inc(S["coef"], 1)
        dve.wait_ge(S["coef"], 3)

        def bnt(g, b):
            dve.wait_ge(S["x2l"], (g + 1) * 16)
            nc.vector.tensor_scalar(BNT[b][:, :], X2T[b][:, :], ab[:, 0:1], ab[:, 1:2], ALU.mult, ALU.add).then_inc(S["bnt"], 1)

        def choose(part, j, r, q):
            if part == 0:
                await_(dve, S["sim"], j + 1)
            if part < 4:
                for e in range(4 * part, 4 * part + 4):
                    o = nc.vector.max(M8[q][:, e // FH, e % FH, :], SIM[r][:, e // FH, e % FH, :])
                if part == 3:
                    o.then_inc(S["m8"], 1)
            if part == 4:
                dve.wait_ge(S["m8"], j + 1)
                x, y = M8[q][:, 0, :, :], M8[q][:, 1, :, :]
                nc.vector.tensor_tensor(CD[:, :, 0:8], x[:, :, 0:1].broadcast_to([P, FH, 8]), y[:, :, :], ALU.add)
                nc.vector.tensor_tensor(CD[:, :, 8:12], x[:, :, 1:2].broadcast_to([P, FH, 4]), y[:, :, 0:4], ALU.add)
                nc.vector.tensor_tensor(CD[:, :, 12:16].rearrange("p h (a b) -> p h a b", a=2),
                                        x[:, :, 2:4].unsqueeze(3).broadcast_to([P, FH, 2, 2]),
                                        y[:, :, 0:2].unsqueeze(2).broadcast_to([P, FH, 2, 2]), ALU.add)
                nc.vector.tensor_tensor(CD[:, :, 16:20], x[:, :, 4:8], y[:, :, 0:1].broadcast_to([P, FH, 4]), ALU.add).then_inc(S["cd"], 1)
            if part == 5:
                await_(dve, S["cd"], j + 1)
                for h in range(FH):
                    o = nc.vector.max(TOP[q][:, h, :], CD[:, h, :])
                o.then_inc(S["top"], 1)
                dve.wait_ge(S["top"], j + 1)
                nc.vector.tensor_tensor(D8[:, :, :], TOP[q][:, :, :], TOP[q][:, :, 0:1].broadcast_to([P, FH, TOPK]), ALU.subtract).then_inc(S["d8"], 1)
            if part == 6:
                dve.wait_ge(S["e8"], j + 1)
                nc.vector.tensor_reduce(Z[:, :], E8[:, :, :], AX.X, ALU.add).then_inc(S["z"], 1)
            if part == 7:
                dve.wait_ge(S["lz"], j + 1)
                nc.vector.scalar_tensor_tensor(out=NB[q][:, :], in0=LZ[:, :], scalar=-1.0, in1=TOP[q][:, :, 0], op0=ALU.mult, op1=ALU.subtract).then_inc(S["nb"], 1)

        bnt(0, 0)
        for part in range(8):
            choose(part, 0, 0, 0)

        def experts(j, g, b, k):
            dve.wait_ge(S["turned"], (j + 1) * FH)
            dve.wait_ge(S["ge"], (g + 1) * BLK)
            wait_pos(dve, S["outp"], j - 1)
            nc.vector.tensor_tensor(CT[k % 2][:, :, :], WT[k % 2][:, :, :], GE[b][:, :, k * P:(k + 1) * P], ALU.mult).then_inc(S["ct"], 1)

        def finish(j, g, b, k):
            dve.wait_ge(S["outp"], j + 1)
            dve.wait_ge(S["x1l"], (g + 1) * 16)
            wait_pos(dve, S["stored"], (g - 1) * 16)
            nc.vector.tensor_tensor(OUT[b][:, k, :], POUT[:, (k % 4) * P:(k % 4 + 1) * P], X1[b][:, k, :], ALU.add).then_inc(S["outs"], 1)

        def group(g, b, more):
            for k in range(GT):
                j = g * GT + k
                q = k % 2
                prev = (j - 1, g, b, k - 1) if k else (j - 1, g - 1, 1 - b, GT - 1)
                real = not (isinstance(j, int) and j == 0)
                for h in range(FH):
                    if more or k < GT - 1:
                        choose(h, j + 1, (k + 1) % 4, 1 - q)
                    if h == 1 and k == 1 and more:
                        bnt(g + 1, 1 - b)
                    if h == 1 and real:
                        experts(*prev)
                    if h == 4 and real:
                        finish(*prev)
                    if h in VSUM:
                        sum_buffer_free(dve, j, h)
                        pair_sums(nc.vector, j, h, k).then_inc(S["vsum"], 1)
                    dve.wait_ge(S["e"], j * FH + h + 1)
                    nc.vector.scalar_tensor_tensor(out=W[h % RING][:, :], in0=SUM[h % RING][:, :], scalar=TOP[q][:, h, TOPK - 1:TOPK],
                                                   in1=W[h % RING][:, :], op0=ALU.is_ge, op1=ALU.mult).then_inc(S["masked"], 1)

        steps(dve, group)
        last = (GROUPS * GT - 1, GROUPS - 1, 1, GT - 1)
        experts(*last)
        finish(*last)

    @block.tensor
    def _(pe):
        def similar(j, g, b, k):
            pe.wait_ge(S["bnt"], g + 1)
            wait_pos(pe, S["sim"], j)
            pe.matmul(PSIM[:, :], BNT[b][:, k * P:(k + 1) * P], KM[:, :], start=True, stop=True).then_inc(S["sim_p"], 1)

        def o_block(g, b, e):
            pe.wait_ge(S["x2l"], (g + 1) * 16)
            wait_pos(pe, S["ge"], g * BLK + e - 1)
            pe.matmul(PO[e % 2][:, :], key_in[:, e * P:(e + 1) * P], X2T[b][:, :], start=True, stop=True).then_inc(S["o_p"], 1)

        for e in range(BLK):
            o_block(0, 0, e)
        similar(0, 0, 0, 0)
        similar(1, 0, 0, 1)

        def outputs(j, k):
            pe.wait_ge(S["ct"], j + 1)
            wait_pos(pe, S["outs"], j - 3)
            for e in range(BLK):
                o = pe.matmul(POUT[:, (k % 4) * P:(k % 4 + 1) * P], CT[k % 2][:, e, :], key_out[:, e, :], start=(e == 0), stop=(e == BLK - 1))
            o.then_inc(S["outp"], 1)

        def group(g, b, more):
            for k in range(GT):
                j = g * GT + k
                real = not (isinstance(j, int) and j == 0)
                for h in range(FH):
                    if h == 1 and (more or k < 2):
                        if k < 2:
                            similar(j + 2, g, b, k + 2)
                        else:
                            similar(j + 2, g + 1, 1 - b, k - 2)
                    if k == 2 and more and h == 0:
                        for e in range(BLK):
                            o_block(g + 1, 1 - b, e)
                    if h == 3 and real:
                        outputs(j - 1, (k - 1) % GT)
                    pe.wait_ge(S["masked"], j * FH + h + 1)
                    if h == 0:
                        wait_pos(pe, S["ct"], j - 1)
                    for e in range(BLK):
                        o = pe.matmul(WT[k % 2][:, e, :], W[h % RING][:, e * P:(e + 1) * P], ident[:, :], is_transpose=True,
                                      start=(h == 0 and e % 4 == 0), stop=(h == FH - 1), skip_group_check=True)
                    o.then_inc(S["turned"], 1)

        steps(pe, group)
        outputs(GROUPS * GT - 1, GT - 1)


def program(nc, x, w_qkvT, w_projT, ident, identb, band, w_q, keysT, key_inT, key_out, gb, out):
    x1 = nc.dram_tensor("x1", (SEQS * T, P), F32, kind="Internal").ap()
    x2T = nc.dram_tensor("x2T", (P, SEQS * T), F32, kind="Internal").ap()
    with ExitStack() as both:
        def sb(name, shape):
            return both.enter_context(nc.sbuf_tensor(name, shape, F32))

        idf = sb("idf", [P, P])
        KI = sb("KI", [P, NE])
        KO = sb("KO", [P, BLK, P])
        KM = sb("KM", [P, 2 * FH * NK])
        GB = sb("GB", [P, 2])
        bnst = sb("bnst", [P, SEQS, 6])
        extra = [(idf[:, :], ident), (KI[:, :], key_inT), (KO[:, :, :], key_out), (GB[:, :], gb)]
        with ExitStack() as ctx:
            attention(nc, ctx, x, w_qkvT, w_projT, identb, band, w_q, keysT, idf, bnst, KM, extra, x1, x2T)
        with ExitStack() as ctx:
            ffn(nc, ctx, x1, x2T, KM, KI, KO, GB, idf, bnst, out)


def kernel(L0_attn_x, L0_attn_w_qkv, L0_attn_w_proj, L0_ffn_gamma, L0_ffn_beta, L0_ffn_w_q, L0_ffn_keys,
           L0_ffn_key_in, L0_ffn_key_out):
    import ml_dtypes
    import numpy as np
    import concourse.bacc as bacc
    from concourse.bass_utils import run_bass_kernel_spmd

    w = np.asarray(L0_attn_w_qkv).reshape(3, P, P)
    dh = [w[n].reshape(H, DK, P).transpose(1, 0, 2).reshape(P, P) for n in range(2)]
    keep = np.arange(P)[None, :] >= np.arange(P)[:, None]
    arrays = {
        "x": np.asarray(L0_attn_x).reshape(SEQS * T, P),
        "w_qkvT": np.concatenate([dh[0].T, dh[1].T, w[2].T], axis=1),
        "w_projT": np.asarray(L0_attn_w_proj).T,
        "ident": np.eye(P, dtype=np.float32),
        "identb": np.eye(P, dtype=np.float32).astype(ml_dtypes.bfloat16),
        "band": np.concatenate([np.where(keep, 0, -1e30), np.where(keep.T, 0, -1e30)], axis=1).astype(ml_dtypes.bfloat16),
        "w_q": np.asarray(L0_ffn_w_q),
        "keysT": np.asarray(L0_ffn_keys).transpose(3, 2, 0, 1).reshape(P, 2 * FH * NK),
        "key_inT": np.asarray(L0_ffn_key_in).T,
        "key_out": np.asarray(L0_ffn_key_out).reshape(BLK, P, P).transpose(1, 0, 2),
        "gb": np.stack([np.asarray(L0_ffn_gamma), np.asarray(L0_ffn_beta)], axis=1),
    }
    arrays = {name: np.ascontiguousarray(a) for name, a in arrays.items()}
    nc = bacc.Bacc("TRN2", target_bir_lowering=False, num_devices=1)
    args = {name: nc.dram_tensor("in_" + name, a.shape, mybir.dt.from_np(a.dtype), kind="ExternalInput").ap()
            for name, a in arrays.items()}
    out = nc.dram_tensor("out_0", (SEQS * T, P), F32, kind="ExternalOutput").ap()
    program(nc, out=out, **args)
    ran = run_bass_kernel_spmd(nc, [{"in_" + name: a for name, a in arrays.items()}], core_ids=[0])
    return ran.results[0]["out_0"].reshape(SEQS, T, P)
```

```python
from contextlib import ExitStack

import numpy as np
import concourse.bass as bass
from concourse import mybir

F32 = mybir.dt.float32
BF16 = mybir.dt.bfloat16
ACT = mybir.ActivationFunctionType
ALU = mybir.AluOpType
AX = mybir.AxisListType

P = 128
SEQS = 16
T = 512
TILES = T // P
H = 16
DK = P // H
EPS = 1e-5
TERMS = 9
KQ = TERMS * DK
SHIFT = 3
TWO_ONES = float(np.array([0x3F803F80], np.uint32).view(np.float32)[0])
SLOT_V, SLOT_PT = 32, 1280


def attention(nc, ctx, x, w_qkvT, w_projT, identb, band, w_q, keysT, idf, bnst, KM, extra, x1_out, x2T_out):
    def sb(name, shape, dt=F32):
        return ctx.enter_context(nc.sbuf_tensor(name, shape, dt))

    def ps(name, shape, dt=F32):
        return ctx.enter_context(nc.psum_tensor(name, shape, dt))

    def sem(name):
        return ctx.enter_context(nc.semaphore(name))

    xs = x.rearrange("(s i p) c -> s p i c", i=TILES, p=P)
    x1s = x1_out.rearrange("(s i p) c -> s p i c", i=TILES, p=P)
    x2Ts = x2T_out.rearrange("c (s n) -> s c n", n=T)
    q_parts = nc.dram_tensor("q_parts", (3, P, T), BF16, kind="Internal").ap()
    k_parts = nc.dram_tensor("k_parts", (3, P, T), BF16, kind="Internal").ap()

    m_parts = nc.dram_tensor("m_parts", (3, H, T), BF16, kind="Internal").ap()

    wq = sb("wq", [P, 3 * P])
    wp = sb("wp", [P, P])
    WQF = sb("WQF", [P, 2 * FH, P])
    KT = sb("KT", [P, 2 * FH * NK])
    idb = sb("idb", [P, P], BF16)
    bandb = sb("bandb", [P, 2 * P], BF16)
    xin = [sb(f"xin{b}", [P, TILES, P]) for b in range(2)]
    xres = sb("xres", [P, TILES, P])
    st6 = sb("st6", [P, TILES, 6])
    mv = sb("mv", [P, TILES, 2])
    ve = sb("ve", [P, TILES])
    half = sb("half", [P, TILES])
    rs = sb("rs", [P, TILES])
    xn = sb("xn", [P, TILES, P])
    xnT = [sb(f"xnT{b}", [P, T]) for b in range(2)]
    qp = sb("qp", [P, 3, T], BF16)
    kp = sb("kp", [P, 3, T], BF16)
    rq = sb("rq", [P, T])
    rk = sb("rk", [P, T])
    Q = [sb(f"Q{b}", [P, H, T], BF16) for b in range(2)]
    K = [sb(f"K{b}", [P, H, T], BF16) for b in range(2)]
    V = [sb(f"V{b}", [P, TILES, H, SLOT_V]) for b in range(2)]
    mx = sb("mx", [P, H, TILES])
    mp = sb("mp", [H // 2, 3, T], BF16)
    rm = sb("rm", [H // 2, T])
    PT = sb("PT", [P, 8, SLOT_PT])
    U = [sb(f"U{b}", [P, 4, T]) for b in range(2)]
    rec = sb("rec", [P, TILES, H])
    A = sb("A", [P, TILES, P])
    AT = sb("AT", [P, T])
    X1 = sb("X1", [P, TILES, P])
    t6 = sb("t6", [P, TILES, 6])
    tv = sb("tv", [P, TILES, 2])
    te = sb("te", [P, TILES])
    trs = sb("trs", [P, TILES])
    X2 = sb("X2", [P, TILES, P])
    X2T = sb("X2T", [P, T])

    SX = ps("SX", [P, 2, 256])
    SY = ps("SY", [P, 2, 512])
    TX = ps("TX", [P, 2, 256])
    TY = ps("TY", [P, 2, 512])
    PV = ps("PV", [P, T])
    MB = ps("MB", [P, TILES, P])

    names = ("passed wrote_m memory km_p km_r consts ones kones ve_r rs_r xload xn_r xnT_p xnT_r q_p q1 q_r q2 q3 k_p k1 k_r k2 k3 v_p v_r "
             "wrote_q wrote_k back0 back1 sx sy sx_u sy_u tx ty tx_u ty_u masked pvm pv_u "
             "mt_p m1 m_r m2 m3 mrow att_p att_u at_p at_u pj_p x1_r te_r trs_r x2_r x2T_p x2T_r bn_r "
             "xres_l st_x1 st_x2 dv1 dv2 dv3 dv4 dv5 bn_all").split()
    S = {n: sem("a_" + n) for n in names}

    def steps(eng, do):
        for t in (-1, 0, 1):
            do(t, t)
        with eng.Fori(0, 6) as i:
            do(i * 2 + 2, 2)
            do(i * 2 + 3, 3)
        for t in (14, 15, 16, 17):
            do(t, t)

    def live(c, n):
        return 0 <= c < SEQS

    SHARED = [(1, "mt1", -1, "m_r", 2, 2), (3, "att0", -2, "att_u", 4, 1), (4, "xnT", 1, "xnT_r", 1, 1),
              (5, "q", 1, "q_r", 1, 1), (6, "k", 1, "k_r", 1, 1), (7, "att1", -2, "att_u", 4, 2), (8, "att2", -2, "att_u", 4, 3),
              (9, "mt0", 0, "m_r", 2, 1), (10, "att3", -2, "att_u", 4, 4), (11, "at", -2, "at_u", 1, 1),
              (12, "pj", -2, "x1_r", 1, 1), (13, "v", 0, "v_r", 1, 1), (15, "x2T", -2, "x2T_r", 1, 1)]
    ORDER = [n for _, n, *_ in SHARED]

    def bank_free(pe, name, t, c):
        at = ORDER.index(name)
        for back in range(1, len(SHARED) + 1):
            j, dt = (at - back) % len(SHARED), -1 if back > at else 0
            _, _, off, sname, per, nth = SHARED[j]
            if 0 <= c + dt + off < SEQS:
                pe.wait_ge(S[sname], (t + dt + off) * per + nth)
                return

    def await_(eng, semaphore, count):
        eng.wait_ge(semaphore, count)
        eng.sem_inc(S["passed"], 1)

    def one(ap, s):
        return ap[s]

    block = ctx.enter_context(nc.Block())

    @block.sync
    def _(sp):
        sp.dma_start(xin[0][:, :, :], xs[0]).then_inc(S["xload"], 16)
        for dst, src in ((wq[:, :], w_qkvT), (wp[:, :], w_projT), (idb[:, :], identb), (bandb[:, :], band)):
            sp.dma_start(dst, src).then_inc(S["consts"], 16)
        for dst, src in extra[:1]:
            sp.dma_start(dst, src).then_inc(S["consts"], 16)
        sp.wait_ge(S["xload"], 16)
        sp.dma_start(xin[1][:, :, :], xs[1]).then_inc(S["xload"], 16)
        sp.wait_ge(S["xload"], 32)
        for dst, src in [(WQF[:, :, :], w_q.rearrange("(g k) d -> k g d", k=P)), (KT[:, :], keysT)] + extra[1:]:
            sp.dma_start(dst, src).then_inc(S["memory"], 16)
        def back(t, half_, b):
            hs = slice(8 * half_, 8 * half_ + 8)
            to = S["back0"] if half_ == 0 else S["back1"]
            for a in range(3):
                sp.dma_start(K[b][24 * a:24 * a + 24, hs, :],
                             k_parts.rearrange("a (d h) n -> (a d) h n", h=H)[:, hs, :]).then_inc(to, 16)
                for e in range(3):
                    r = 24 * a + 8 * e
                    sp.dma_start(Q[b][r:r + 8, hs, :],
                                 q_parts[a].rearrange("(d h) n -> d h n", h=H)[:, hs, :]).then_inc(to, 16)

        def shift_rows(t, half_, b):
            hs = slice(8 * half_, 8 * half_ + 8)
            sp.dma_start(m_parts[:, hs, :].rearrange("r h n -> h r n"), mp[:, :, :]).then_inc(S["wrote_m"], 16)
            await_(sp, S["wrote_m"], 16 * (2 * t + half_ + 1))
            sp.dma_start(Q[b][KQ:KQ + 3, hs, :], m_parts[:, hs, :]).then_inc(S["mrow"], 16)

        def step(t, c):
            if 0 <= c - 2 < SEQS:
                if c - 3 >= 0:
                    await_(sp, S["x1_r"], t - 2)
                sp.dma_start(xres[:, :, :], one(xs, t - 2)).then_inc(S["xres_l"], 16)
            if 0 <= c - 1 < SEQS:
                await_(sp, S["m3"], (t - 1) * 2 + 2)
                shift_rows(t - 1, 1, (c - 1) % 2)
            if 0 <= c + 1 < SEQS:
                await_(sp, S["q3"], t + 2)
                if c >= 0:
                    await_(sp, S["back0"], 16 * 12 * (t + 1))
                    await_(sp, S["back1"], 16 * 12 * (t + 1))
                sp.dma_start(q_parts.rearrange("a p n -> p a n"), qp[:, :, :]).then_inc(S["wrote_q"], 16)
                await_(sp, S["k3"], t + 2)
                sp.dma_start(k_parts.rearrange("a p n -> p a n"), kp[:, :, :]).then_inc(S["wrote_k"], 16)
                await_(sp, S["wrote_q"], 16 * (t + 2))
                await_(sp, S["wrote_k"], 16 * (t + 2))
                if c - 1 >= 0:
                    await_(sp, S["ty"], (t - 1) * H + 8)
                if c >= 0 and c + 2 < SEQS:
                    sp.dma_start(xin[c % 2][:, :, :], one(xs, t + 2)).then_inc(S["xload"], 16)
                if c <= 0:
                    sp.wait_ge(S["kones"], c + 2)
                back(t + 1, 0, (c + 1) % 2)
            if 0 <= c < SEQS:
                await_(sp, S["m3"], t * 2 + 1)
                shift_rows(t, 0, c % 2)
            if 0 <= c - 2 < SEQS:
                await_(sp, S["x1_r"], t - 1)
                sp.dma_start(one(x1s, t - 2), X1[:, :, :]).then_inc(S["st_x1"], 16)
                await_(sp, S["x2T_r"], t - 1)
                sp.dma_start(one(x2Ts, t - 2), X2T[:, :]).then_inc(S["st_x2"], 16)
            if 0 <= c + 1 < SEQS:
                if c - 1 >= 0:
                    await_(sp, S["ty"], (t - 1) * H + 16)
                back(t + 1, 1, (c + 1) % 2)

        steps(sp, step)
        await_(sp, S["st_x1"], 16 * SEQS)
        await_(sp, S["st_x2"], 16 * SEQS)

    @block.gpsimd
    def _(pool):
        nc.gpsimd.memset(half[:, :], -0.5).then_inc(S["ones"], 1)
        for b in range(2):
            nc.gpsimd.memset(V[b][:, :, :, :], 0.0).then_inc(S["ones"], 1)
        pool.wait_ge(S["ones"], 3)
        for b in range(2):
            nc.gpsimd.memset(V[b][:, :, :, DK:DK + 1], 1.0).then_inc(S["ones"], 1)

        def mask(out, pairs, stop_low):
            s = 1 if stop_low else -1
            nc.gpsimd
            return nc.gpsimd.affine_select(out=out, in_=out, compare_op=ALU.is_ge, fill=0.0, base=0,
                                           pattern=([[0, 2]] if pairs else []) + [[s, P]], channel_multiplier=-s)

        def step(t, c):
            for h in range(H):
                if h == 1 and 0 <= c + 1 < SEQS:
                    pool.wait_ge(S["ve_r"], t + 2)
                    nc.gpsimd.tensor_tensor(rs[:, :], ve[:, :], half[:, :], ALU.pow).then_inc(S["rs_r"], 1)
                if 0 <= c - 1 < SEQS:
                    pt = PT[:, h % 8, :]
                    y = pt[:, 512:1280].rearrange("p (j n) -> p j n", j=2)
                    await_(pool, S["tx_u"], (t - 1) * H + h + 1)
                    mask(pt[:, 128:256], False, False).then_inc(S["masked"], 1)
                    mask(pt[:, 256:384], False, True).then_inc(S["masked"], 1)
                    await_(pool, S["ty_u"], (t - 1) * H + h + 1)
                    mask(y[:, :, 0:128], True, True).then_inc(S["masked"], 1)
                    mask(y[:, :, 256:384], True, False).then_inc(S["masked"], 1)
                if h == 13 and 0 <= c - 2 < SEQS:
                    pool.wait_ge(S["te_r"], t - 1)
                    nc.gpsimd.tensor_tensor(trs[:, :], te[:, :], half[:, :], ALU.pow).then_inc(S["trs_r"], 1)

        steps(pool, step)

    @block.scalar
    def _(act):
        act.wait_ge(S["ones"], 5)

        def step(t, c):
            b = c % 2
            for h in range(H):
                if h == 1 and 0 <= c - 1 < SEQS:
                    shift(t - 1, 2)
                if h == 9 and 0 <= c < SEQS:
                    shift(t, 1)
                if h == 4 and 0 <= c + 1 < SEQS:
                    act.wait_ge(S["xnT_p"], t + 2)
                    if c - 1 >= 0:
                        act.wait_ge(S["v_p"], t)
                    nc.scalar.copy(xnT[1 - b][:, :].rearrange("p (i n) -> p i n", n=P), MB[:, :, :]).then_inc(S["xnT_r"], 1)
                for hh, nm, src, dst, r, sc in ((5, "q", MB, qp, rq, DK ** -0.5), (6, "k", MB, kp, rk, 1.0)):
                    if h == hh and 0 <= c + 1 < SEQS:
                        act.wait_ge(S[nm + "_p"], t + 2)
                        if c >= 0:
                            act.wait_ge(S["wrote_" + nm], 16 * (t + 1))
                        nc.scalar.mul(dst[:, 0, :].rearrange("p (i n) -> p i n", n=P), src[:, :, :], sc).then_inc(S[nm + "1"], 1)
                    if h == hh + 1 and 0 <= c + 1 < SEQS:
                        act.wait_ge(S[nm + "_r"], t + 2)
                        nc.scalar.copy(dst[:, 1, :], r[:, :]).then_inc(S[nm + "2"], 1)
                if h == 8 and c == -1:
                    act.wait_ge(S["km_p"], 1)
                    nc.scalar.copy(KM[:, :], MB[:, :, :].rearrange("p i n -> p (i n)")).then_inc(S["km_r"], 1)
                if h == 13 and 0 <= c < SEQS:
                    act.wait_ge(S["v_p"], t + 1)
                    if c >= 2:
                        act.wait_ge(S["pvm"], (t - 1) * 4)
                    nc.scalar.copy(V[b][:, :, :, 0:DK], MB[:, :, :].rearrange("p i (h d) -> p i h d", d=DK)).then_inc(S["v_r"], 1)
                for g, (sl, ds_) in enumerate(((6, 1), (10, 1), (14, 1), (2, 2))):
                    if h == sl and 0 <= c - ds_ < SEQS:
                        act.wait_ge(S["pvm"], (t - ds_) * 4 + g + 1)
                        if c - ds_ >= 2:
                            act.wait_ge(S["att_p"], (t - ds_ - 1) * 4)
                        nc.scalar.copy(U[(c - ds_) % 2][:, g, :], PV[:, :]).then_inc(S["pv_u"], 1)
                if h == 11 and 0 <= c - 2 < SEQS:
                    act.wait_ge(S["at_p"], t - 1)
                    nc.scalar.copy(AT[:, :].rearrange("p (i n) -> p i n", n=P), MB[:, :, :]).then_inc(S["at_u"], 1)
                if h == 15 and 0 <= c - 2 < SEQS:
                    act.wait_ge(S["x2T_p"], t - 1)
                    if c - 2 >= 1:
                        act.wait_ge(S["st_x2"], 16 * (t - 2))
                        act.wait_ge(S["bn_r"], t - 2)
                    nc.scalar.copy(X2T[:, :].rearrange("p (i n) -> p i n", n=P), MB[:, :, :]).then_inc(S["x2T_r"], 1)
                if 0 <= c - 1 < SEQS:
                    pt = PT[:, h % 8, :]
                    n = (t - 1) * H + h + 1
                    act.wait_ge(S["tx"], n)
                    if h >= 8:
                        act.wait_ge(S["pvm"], (t - 1) * 4 + (h - 8) // 4 + 1)
                    elif c - 1 >= 1:
                        act.wait_ge(S["pvm"], (t - 2) * 4 + 2 + h // 4 + 1)
                    nc.scalar.activation(pt[:, 0:512], TX[:, :, :].rearrange("p j n -> p (j n)"), ACT.Exp).then_inc(S["tx_u"], 1)
                    act.wait_ge(S["ty"], n)
                    nc.scalar.activation(pt[:, 512:1280].rearrange("p (j n) -> p j n", j=2), TY[:, :, 0:384], ACT.Exp).then_inc(S["ty_u"], 1)

        def shift(s, nth):
            act.wait_ge(S["mt_p"], s * 2 + nth)
            prev = (s * 2 + nth - 1)
            if not isinstance(prev, int) or prev >= 1:
                act.wait_ge(S["mrow"], prev * 16)
            nc.scalar.mul(mp[:, 0, :].rearrange("p (i n) -> p i n", n=P), MB[0:8, :, :], -1.0).then_inc(S["m1"], 1)
            act.wait_ge(S["m_r"], s * 2 + nth)
            nc.scalar.copy(mp[:, 1, :], rm[:, :]).then_inc(S["m2"], 1)

        steps(act, step)

    @block.vector
    def _(dve):

        def stats(part, s, src, a6, av, ae, s1, s2, to):
            if part == 0:
                for i in range(TILES):
                    nc.vector.bn_stats(a6[:, i, :], src[:, i, :]).then_inc(s1, 1)
                return
            await_(dve, s1, (s + 1) * TILES)
            for i in range(TILES):
                nc.vector.bn_aggr(av[:, i, :], a6[:, i, :]).then_inc(s2, 1)
            dve.wait_ge(s2, (s + 1) * TILES)
            nc.vector.tensor_scalar(ae[:, :], av[:, :, 1], EPS, None, ALU.add).then_inc(to, 1)

        def norm(src, av, r, dst, to):
            for i in range(TILES):
                o = nc.vector.tensor_scalar(dst[:, i, :], src[:, i, :], av[:, i, 0:1], r[:, i:i + 1], ALU.subtract, ALU.mult)
            o.then_inc(to, 1)

        def shift(s, nth):
            dve.wait_ge(S["m1"], s * 2 + nth)
            nc.vector.scalar_tensor_tensor(out=rm[:, :].rearrange("p (i n) -> p i n", n=P), in0=MB[0:8, :, :], scalar=-1.0,
                                           in1=mp[:, 0, :].rearrange("p (i n) -> p i n", n=P), op0=ALU.mult, op1=ALU.subtract).then_inc(S["m_r"], 1)
            dve.wait_ge(S["m2"], s * 2 + nth)
            nc.vector.tensor_tensor(mp[:, 2, :], rm[:, :], mp[:, 1, :], ALU.subtract).then_inc(S["m3"], 1)

        def step(t, c):
            b = c % 2
            for h in range(H):
                if 0 <= c < SEQS:
                    n = t * H + h + 1
                    dve.wait_ge(S["sx"], n)
                    if h == 0 and c >= 1:
                        dve.wait_ge(S["mt_p"], t * 2 - 1)
                    if h == 8 and c >= 1:
                        dve.wait_ge(S["mt_p"], t * 2)
                    nc.vector.tensor_reduce(mx[:, h, 0:4:3], SX[:, :, :], AX.X, ALU.max).then_inc(S["sx_u"], 1)
                    dve.wait_ge(S["sy"], n)
                    nc.vector.tensor_reduce(mx[:, h, 1:3], SY[:, :, 0:384], AX.X, ALU.max).then_inc(S["sy_u"], 1)
                if h == 1 and 0 <= c - 1 < SEQS:
                    shift(t - 1, 2)
                if h == 9 and 0 <= c < SEQS:
                    shift(t, 1)
                if h == 0 and 0 <= c + 1 < SEQS:
                    dve.wait_ge(S["xload"], 16 * (t + 2))
                    stats(0, t + 1, xin[1 - b], st6, mv, ve, S["dv1"], S["dv2"], S["ve_r"])
                if h == 1 and 0 <= c + 1 < SEQS:
                    stats(1, t + 1, xin[1 - b], st6, mv, ve, S["dv1"], S["dv2"], S["ve_r"])
                if h == 3 and 0 <= c + 1 < SEQS:
                    dve.wait_ge(S["rs_r"], t + 2)
                    if c >= 0:
                        dve.wait_ge(S["xnT_p"], t + 1)
                    norm(xin[1 - b], mv, rs, xn, S["xn_r"])
                if c == -1 and h in (4, 7):
                    both = K[0 if h == 4 else 1][64:P, :, :].rearrange("p h n -> p (h n)").bitcast(F32)
                    nc.vector.memset(both, TWO_ONES).then_inc(S["kones"], 1)
                for hh, nm, dst, r, sc in ((5, "q", qp, rq, DK ** -0.5), (6, "k", kp, rk, 1.0)):
                    if h == hh and 0 <= c + 1 < SEQS:
                        dve.wait_ge(S[nm + "1"], t + 2)
                        nc.vector.scalar_tensor_tensor(out=r[:, :].rearrange("p (i n) -> p i n", n=P), in0=MB[:, :, :], scalar=sc,
                                                       in1=dst[:, 0, :].rearrange("p (i n) -> p i n", n=P),
                                                       op0=ALU.mult, op1=ALU.subtract).then_inc(S[nm + "_r"], 1)
                    if h == hh + 1 and 0 <= c + 1 < SEQS:
                        dve.wait_ge(S[nm + "2"], t + 2)
                        nc.vector.tensor_tensor(dst[:, 2, :], r[:, :], dst[:, 1, :], ALU.subtract).then_inc(S[nm + "3"], 1)
                for i, sl in enumerate((3, 7, 8, 10)):
                    if h == sl and 0 <= c - 2 < SEQS:
                        n = (t - 2) * 4 + i + 1
                        dve.wait_ge(S["att_p"], n)
                        hv = MB[:, :, :].rearrange("p g (h e) -> p (g h) e", e=SLOT_V)
                        nc.vector.reciprocal(rec[:, i, :], hv[:, :, DK]).then_inc(S["dv3"], 1)
                        dve.wait_ge(S["dv3"], n)
                        nc.vector.tensor_tensor(A[:, i, :].rearrange("p (h d) -> p h d", d=DK), hv[:, :, 0:DK],
                                                rec[:, i, :].unsqueeze(2).broadcast_to([P, H, DK]), ALU.mult).then_inc(S["att_u"], 1)
                if h == 12 and 0 <= c - 2 < SEQS:
                    dve.wait_ge(S["pj_p"], t - 1)
                    dve.wait_ge(S["xres_l"], 16 * (t - 1))
                    if c - 2 >= 1:
                        dve.wait_ge(S["st_x1"], 16 * (t - 2))
                    nc.vector.tensor_tensor(X1[:, :, :], MB[:, :, :], xres[:, :, :], ALU.add).then_inc(S["x1_r"], 1)
                if h == 13 and 0 <= c - 2 < SEQS:
                    dve.wait_ge(S["x1_r"], t - 1)
                    stats(0, t - 2, X1, t6, tv, te, S["dv4"], S["dv5"], S["te_r"])
                    stats(1, t - 2, X1, t6, tv, te, S["dv4"], S["dv5"], S["te_r"])
                if h == 14 and 0 <= c - 2 < SEQS:
                    dve.wait_ge(S["trs_r"], t - 1)
                    norm(X1, tv, trs, X2, S["x2_r"])
            if 0 <= c - 2 < SEQS:
                dve.wait_ge(S["x2T_r"], t - 1)
                nc.vector.bn_stats(bnst[:, t - 2, :] if isinstance(t, int) else bnst[:, bass.ds(t - 2, 1), :].rearrange("p o n -> p (o n)"), X2T[:, :]).then_inc(S["bn_r"], 1)

        steps(dve, step)

    @block.tensor
    def _(pe):
        pe.wait_ge(S["consts"], 80)
        pe.wait_ge(S["ones"], 5)
        HI, LO = bandb[:, 0:P], bandb[:, P:2 * P]

        def scores(t, c, h):
            b, n = c % 2, t * H + h + 1
            if h == 0:
                pe.wait_ge(S["back0"], 192 * (t + 1))
            if h == 8:
                pe.wait_ge(S["back1"], 192 * (t + 1))

            def tile(out, i, k0, k1, clear=True):
                pe.matmul(out, Q[b][0:KQ, h, i * P:(i + 1) * P], K[b][0:KQ, h, k0 * P:k1 * P],
                          start=clear, stop=False, skip_group_check=True)

            def outside(out, band_):
                return pe.matmul(out, idb[:, :], band_, start=False, stop=True, skip_group_check=True)

            if c > 0 or h > 0:
                pe.wait_ge(S["sx_u"], n - 1)
            tile(SX[:, 0, :], 0, 0, 2)
            tile(SX[:, 1, :], 3, 2, 4, False)
            outside(SX[:, :, :].rearrange("p j n -> p (j n)")[:, P:3 * P], bandb[:, :]).then_inc(S["sx"], 1)
            if c > 0 or h > 0:
                pe.wait_ge(S["sy_u"], n - 1)
            for n, i in enumerate((1, 2)):
                tile(SY[:, n, 0:3 * P], i, i - 1, i + 2)
                outside(SY[:, n, 0:P], LO)
                o = outside(SY[:, n, 2 * P:3 * P], HI)
            o.then_inc(S["sy"], 1)

        def scoresT(t, c, h):
            s = t - 1
            b, n = (c - 1) % 2, s * H + h + 1
            R = KQ + SHIFT
            if h == 0:
                pe.wait_ge(S["mrow"], 32 * s + 16)
            if h == 8:
                pe.wait_ge(S["mrow"], 32 * s + 32)

            def tile(out, j, q0, q1):
                return pe.matmul(out[:, 0:(q1 - q0) * P], K[b][0:R, h, j * P:(j + 1) * P], Q[b][0:R, h, q0 * P:q1 * P],
                                 start=True, stop=True, skip_group_check=True)

            if c > 1 or h > 0:
                pe.wait_ge(S["tx_u"], n - 1)
            tile(TX[:, 0, :], 0, 0, 2)
            tile(TX[:, 1, :], 3, 2, 4).then_inc(S["tx"], 1)
            if c > 1 or h > 0:
                pe.wait_ge(S["ty_u"], n - 1)
            tile(TY[:, 0, :], 1, 0, 3)
            tile(TY[:, 1, :], 2, 1, 4).then_inc(S["ty"], 1)

        SPAN = [(0, 0, 2), (512, 0, 3), (896, 1, 4), (256, 2, 4)]

        def values(s, c, g):
            b = c % 2
            pe.wait_ge(S["masked"], (s * H + 4 * g + 4) * 4)
            if g == 0:
                pe.wait_ge(S["v_r"], s + 1)
            if c > 0 or g > 0:
                pe.wait_ge(S["pv_u"], s * 4 + g)
            for j, (at, q0, q1) in enumerate(SPAN):
                for e in range(4):
                    h = 4 * g + e
                    o = pe.matmul(PV[32 * e:32 * e + 32, q0 * P:q1 * P], V[b][:, j, h, :],
                                  PT[:, h % 8, at:at + (q1 - q0) * P], start=(j == 0), stop=(j == 3), skip_group_check=True)
            o.then_inc(S["pvm"], 1)

        def step(t, c):
            b = c % 2
            for h in range(H):
                if 0 <= c < SEQS:
                    scores(t, c, h)
                if h == 1 and 0 <= c - 1 < SEQS:
                    bank_free(pe, "mt1", t, c)
                    pe.wait_ge(S["sy_u"], t * H)
                    for i in range(TILES):
                        o = pe.transpose(MB[0:8, i, :], mx[:, 8:16, i], idf[:, :])
                    o.then_inc(S["mt_p"], 1)
                if h == 9 and 0 <= c < SEQS:
                    bank_free(pe, "mt0", t, c)
                    pe.wait_ge(S["sy_u"], t * H + 8)
                    for i in range(TILES):
                        o = pe.transpose(MB[0:8, i, :], mx[:, 0:8, i], idf[:, :])
                    o.then_inc(S["mt_p"], 1)
                if h == 4 and 0 <= c + 1 < SEQS:
                    bank_free(pe, "xnT", t, c)
                    pe.wait_ge(S["xn_r"], t + 2)
                    for i in range(TILES):
                        o = pe.transpose(MB[:, i, :], xn[:, i, :], idf[:, :])
                    o.then_inc(S["xnT_p"], 1)
                if h == 5 and 0 <= c + 1 < SEQS:
                    bank_free(pe, "q", t, c)
                    pe.wait_ge(S["xnT_r"], t + 2)
                    pe.matmul(MB[:, :, :], wq[:, 0:P], xnT[1 - b][:, :], start=True, stop=True).then_inc(S["q_p"], 1)
                if h == 6 and 0 <= c + 1 < SEQS:
                    bank_free(pe, "k", t, c)
                    pe.matmul(MB[:, :, :], wq[:, P:2 * P], xnT[1 - b][:, :], start=True, stop=True).then_inc(S["k_p"], 1)
                if h == 8 and c == -1:
                    pe.wait_ge(S["memory"], 16 * (2 + len(extra) - 1))
                    pe.wait_ge(S["k_r"], 1)
                    mb = MB[:, :, :].rearrange("p i n -> p (i n)")
                    for g in range(2 * FH):
                        o = pe.matmul(mb[:, g * NK:(g + 1) * NK], WQF[:, g, :], KT[:, g * NK:(g + 1) * NK], start=True, stop=True)
                    o.then_inc(S["km_p"], 1)
                    pe.wait_ge(S["km_r"], 1)
                if h == 13 and 0 <= c < SEQS:
                    bank_free(pe, "v", t, c)
                    for i in range(TILES):
                        o = pe.matmul(MB[:, i, :], xnT[b][:, i * P:(i + 1) * P], wq[:, 2 * P:3 * P], start=True, stop=True)
                    o.then_inc(S["v_p"], 1)
                for i, sl in enumerate((3, 7, 8, 10)):
                    if h == sl and 0 <= c - 2 < SEQS:
                        bank_free(pe, f"att{i}", t, c)
                        pe.wait_ge(S["pv_u"], (t - 1) * 4)
                        for g in range(4):
                            o = pe.transpose(MB[:, g, :], U[b][:, g, i * P:(i + 1) * P], idf[:, :])
                        o.then_inc(S["att_p"], 1)
                if h == 11 and 0 <= c - 2 < SEQS:
                    bank_free(pe, "at", t, c)
                    for i in range(TILES):
                        o = pe.transpose(MB[:, i, :], A[:, i, :], idf[:, :])
                    o.then_inc(S["at_p"], 1)
                if h == 12 and 0 <= c - 2 < SEQS:
                    bank_free(pe, "pj", t, c)
                    for i in range(TILES):
                        o = pe.matmul(MB[:, i, :], AT[:, i * P:(i + 1) * P], wp[:, :], start=True, stop=True)
                    o.then_inc(S["pj_p"], 1)
                if h == 15 and 0 <= c - 2 < SEQS:
                    bank_free(pe, "x2T", t, c)
                    pe.wait_ge(S["x2_r"], t - 1)
                    for i in range(TILES):
                        o = pe.transpose(MB[:, i, :], X2[:, i, :], idf[:, :])
                    o.then_inc(S["x2T_p"], 1)
                for g, (sl, ds_) in enumerate(((6, 1), (10, 1), (14, 1), (2, 2))):
                    if h == sl and 0 <= c - ds_ < SEQS:
                        values(t - ds_, c - ds_, g)
                if 0 <= c - 1 < SEQS:
                    scoresT(t, c, h)

        steps(pe, step)


GROUPS = 16
GT = 4
GN = GT * P
FH = 8
NK = 32
NE = NK * NK
BLK = NE // P
TOPK = 8
CAND = 20
RING = 16
WRING = 8
PARTS = ((0, 1), (2, 3), (4,), (5,), (), (6,), (7,), ())
OSLOT = [(0, 5), (0, 7), (1, 2), (1, 5), (1, 7), (2, 2), (2, 5), (2, 7)]
SIM0 = 3
SSLOT = 4
GSLOT = [(2, 2), (3, 2)]
LEAD = 3



def ffn(nc, ctx, x1, x2T, KM, key_in, key_out, gb, ident, bnst, out):
    def sb(name, shape, dt=F32):
        return ctx.enter_context(nc.sbuf_tensor(name, shape, dt))

    def ps(name, shape, dt=F32):
        return ctx.enter_context(nc.psum_tensor(name, shape, dt))

    def sem(name):
        return ctx.enter_context(nc.semaphore(name))

    x1g = x1.rearrange("(g i p) c -> g p i c", i=GT, p=P)
    outg = out.rearrange("(g i p) c -> g p i c", i=GT, p=P)
    x2Tg = x2T.rearrange("c (g n) -> g c n", n=GN)

    mvb = sb("mvb", [P, 2])
    vb = sb("vb", [P, 1])
    hb = sb("hb", [P, 1])
    rb = sb("rb", [P, 1])
    ab = sb("ab", [P, 2])
    X2T = [sb(f"X2T{b}", [P, GN]) for b in range(2)]
    X1 = [sb(f"X1{b}", [P, GT, P]) for b in range(2)]
    BNT = [sb(f"BNT{b}", [P, GN]) for b in range(2)]
    GE = [sb(f"GE{b}", [P, BLK, GN]) for b in range(2)]
    OUT = [sb(f"OUT{b}", [P, GT, P]) for b in range(2)]
    SIM = [sb(f"SIM{b}", [P, 2, FH, NK]) for b in range(4)]
    M8 = [sb(f"M8{b}", [P, 2, FH, TOPK]) for b in range(2)]
    CD = sb("CD", [P, FH, CAND])
    TOP = [sb(f"TOP{b}", [P, FH, TOPK]) for b in range(2)]
    D8 = sb("D8", [P, FH, TOPK])
    E8 = sb("E8", [P, FH, TOPK])
    Z = sb("Z", [P, FH])
    LZ = sb("LZ", [P, FH])
    NB = [sb(f"NB{b}", [P, FH]) for b in range(2)]
    SUM = [sb(f"SUM{b}", [P, NE]) for b in range(RING)]
    W = [sb(f"W{b}", [P, NE]) for b in range(WRING)]
    CT = [sb(f"CT{b}", [P, BLK, P]) for b in range(2)]

    E = [ps(f"E{b}", [P, NE]) for b in range(2)]
    WT = ps("WT", [P, BLK, P])
    MB = ps("MB2", [P, GN])
    POUT = ps("POUT", [P, P])

    names = ("passed half stat var pow coef x1l x2l bnt sim_p sim psum e masked turned ct outp outs o_p o_r ge stored "
             "m8 cd top d8 e8 z lz nb").split()
    S = {n: sem("f_" + n) for n in names}

    def steps(eng, do):
        do(0, 0, True)
        do(1, 1, True)
        with eng.Fori(1, GROUPS // 2 - 1) as i:
            do(i * 2, 0, True)
            do(i * 2 + 1, 1, True)
        do(GROUPS - 2, 0, True)
        do(GROUPS - 1, 1, False)

    def first(g, b):
        return isinstance(g, int) and g == 0

    def wait_pos(eng, s, v):
        if not isinstance(v, int) or v > 0:
            eng.wait_ge(s, v)

    def await_(eng, semaphore, count):
        eng.wait_ge(semaphore, count)
        eng.sem_inc(S["passed"], 1)

    block = ctx.enter_context(nc.Block())

    @block.sync
    def _(sp):
        sp.dma_start(X2T[0][:, :], x2Tg[0]).then_inc(S["x2l"], 16)
        sp.dma_start(X1[0][:, :, :], x1g[0]).then_inc(S["x1l"], 16)

        def group(g, b, more):
            real = not (isinstance(g, int) and g == 0)
            if more:
                await_(sp, S["x2l"], (g + 1) * 16)
                if real:
                    await_(sp, S["bnt"], g)
                    await_(sp, S["o_r"], g * BLK)
                sp.dma_start(X2T[1 - b][:, :], x2Tg[g + 1]).then_inc(S["x2l"], 16)
            if real:
                store(g - 1, 1 - b)
            if more:
                await_(sp, S["x1l"], (g + 1) * 16)
                sp.dma_start(X1[1 - b][:, :, :], x1g[g + 1]).then_inc(S["x1l"], 16)

        def store(g, b):
            await_(sp, S["outs"], (g + 1) * GT)
            sp.dma_start(outg[g], OUT[b][:, :, :]).then_inc(S["stored"], 16)
            await_(sp, S["stored"], (g + 1) * 16)

        steps(sp, group)
        store(GROUPS - 1, 1)

    def pair_sums(eng, j, h, q):
        sx = SIM[q][:, 0, h, :].unsqueeze(2).broadcast_to([P, NK, NK])
        sy = SIM[q][:, 1, h, :].unsqueeze(1).broadcast_to([P, NK, NK])
        return eng.tensor_tensor(SUM[(q * FH + h) % RING][:, :].rearrange("p (i j) -> p i j", i=NK), sx, sy, ALU.add)

    def sum_buffer_free(eng, j, h):
        wait_pos(eng, S["masked"], j * FH + h - RING + 1)

    @block.gpsimd
    def _(pool):
        nc.gpsimd.memset(hb[:, :], -0.5).then_inc(S["half"], 1)
        pool.wait_ge(S["half"], 1)
        pool.wait_ge(S["var"], 1)
        nc.gpsimd.tensor_tensor(rb[:, :], vb[:, :], hb[:, :], ALU.pow).then_inc(S["pow"], 1)

        def group(g, b, more):
            for k in range(GT):
                j = g * GT + k
                pool.wait_ge(S["sim"], j + 1)
                for h in range(FH):
                    sum_buffer_free(pool, j, h)
                    pair_sums(nc.gpsimd, j, h, k).then_inc(S["psum"], 1)

        steps(pool, group)

    @block.scalar
    def _(act):
        def sim_copy(j, q):
            act.wait_ge(S["sim_p"], j + 1)
            nc.scalar.copy(SIM[q][:, :, :, :].rearrange("p a h k -> p (a h k)"), MB[:, :]).then_inc(S["sim"], 1)

        def gelus(g, b, half):
            act.wait_ge(S["o_r"], g * BLK + (half + 1) * 4)
            o = GE[b][:, 4 * half:4 * half + 4, :].rearrange("p e n -> p (e n)")
            nc.scalar.activation(o, o, ACT.Gelu).then_inc(S["ge"], 1)
            nc.scalar.preload_act_table_set("natural_log_exp_and_others")

        def o_copy(g, b, e):
            act.wait_ge(S["o_p"], g * BLK + e + 1)
            nc.scalar.copy(GE[b][:, e, :], MB[:, :]).then_inc(S["o_r"], 1)

        def bnt(g, b):
            act.wait_ge(S["x2l"], (g + 1) * 16)
            nc.scalar.activation(BNT[b][:, :], X2T[b][:, :], ACT.Identity, scale=ab[:, 0:1], bias=ab[:, 1:2]).then_inc(S["bnt"], 1)

        def finish(j, g, b, k):
            act.wait_ge(S["outp"], j + 1)
            wait_pos(act, S["stored"], (g - 1) * 16)
            nc.scalar.copy(OUT[b][:, k, :], POUT[:, :]).then_inc(S["outs"], 1)

        nc.scalar.preload_act_table_set("gelu_and_others")
        for e in range(BLK):
            if e == SIM0:
                sim_copy(0, 0)
            act.wait_ge(S["o_p"], e + 1)
            nc.scalar.activation(GE[0][:, e, :], E[e // 2 % 2][:, e % 2 * GN:(e % 2 + 1) * GN], ACT.Gelu).then_inc(S["o_r"], 1)
        act.wait_ge(S["o_r"], BLK)
        act.sem_inc(S["ge"], 2)
        nc.scalar.preload_act_table_set("natural_log_exp_and_others")
        sim_copy(1, 1)

        def small_exp(j):
            act.wait_ge(S["d8"], j + 1)
            nc.scalar.activation(E8[:, :, :].rearrange("p h k -> p (h k)"), D8[:, :, :].rearrange("p h k -> p (h k)"), ACT.Exp).then_inc(S["e8"], 1)

        def small_ln(j):
            act.wait_ge(S["z"], j + 1)
            nc.scalar.activation(LZ[:, :], Z[:, :], ACT.Ln).then_inc(S["lz"], 1)

        small_exp(0)
        small_ln(0)

        def group(g, b, more):
            for k in range(GT):
                j = g * GT + k
                q = k % 2
                nxt = more or k < GT - 1
                for h in range(FH):
                    if h == 0:
                        act.wait_ge(S["nb"], j + 1)
                    if h == 5 and k == 1 and more:
                        bnt(g + 1, 1 - b)
                    if h == 1 and not (isinstance(j, int) and j < 2):
                        finish(j - 2, *((g, b, k - 2) if k >= 2 else (g - 1, 1 - b, k + 2)))
                    if h == SSLOT + LEAD and (more or k < 2):
                        wait_pos(act, S["psum"], (j - 1) * FH)
                        sim_copy(j + 2, (k + 2) % 4)
                    then = divmod(k * FH + h - LEAD, FH)
                    if then in OSLOT and more:
                        if then == OSLOT[0]:
                            wait_pos(act, S["ct"], g * GT)
                        o_copy(g + 1, 1 - b, OSLOT.index(then))
                    act.wait_ge(S["psum"], j * FH + h + 1)
                    wait_pos(act, S["masked"], j * FH + h - 1)
                    nc.scalar.activation(E[h % 2][:, :], SUM[(k * FH + h) % RING][:, :], ACT.Exp, bias=NB[q][:, h:h + 1]).then_inc(S["e"], 1)
                    if h == 4 and nxt:
                        small_exp(j + 1)
                    if h == 6 and nxt:
                        small_ln(j + 1)
                    if (k, h) in GSLOT and more:
                        gelus(g + 1, 1 - b, GSLOT.index((k, h)))

        steps(act, group)
        for k in (GT - 2, GT - 1):
            finish((GROUPS - 1) * GT + k, GROUPS - 1, 1, k)

    @block.vector
    def _(dve):
        nc.vector.bn_aggr(mvb[:, :], bnst[:, :, :].rearrange("p s n -> p (s n)")).then_inc(S["stat"], 1)
        dve.wait_ge(S["stat"], 1)
        nc.vector.tensor_scalar(vb[:, :], mvb[:, 1:2], EPS, None, ALU.add).then_inc(S["var"], 1)
        dve.wait_ge(S["pow"], 1)
        nc.vector.tensor_tensor(ab[:, 0:1], rb[:, :], gb[:, 0:1], ALU.mult).then_inc(S["coef"], 1)
        dve.wait_ge(S["coef"], 1)
        nc.vector.tensor_tensor(mvb[:, 1:2], mvb[:, 0:1], ab[:, 0:1], ALU.mult).then_inc(S["coef"], 1)
        dve.wait_ge(S["coef"], 2)
        nc.vector.tensor_tensor(ab[:, 1:2], gb[:, 1:2], mvb[:, 1:2], ALU.subtract).then_inc(S["coef"], 1)
        dve.wait_ge(S["coef"], 3)

        def choose(part, j, r, q):
            if part == 0:
                await_(dve, S["sim"], j + 1)
            if part < 4:
                for e in range(4 * part, 4 * part + 4):
                    o = nc.vector.max(M8[q][:, e // FH, e % FH, :], SIM[r][:, e // FH, e % FH, :])
                if part == 3:
                    o.then_inc(S["m8"], 1)
            if part == 4:
                dve.wait_ge(S["m8"], j + 1)
                x, y = M8[q][:, 0, :, :], M8[q][:, 1, :, :]
                nc.vector.tensor_tensor(CD[:, :, 0:8], x[:, :, 0:1].broadcast_to([P, FH, 8]), y[:, :, :], ALU.add)
                nc.vector.tensor_tensor(CD[:, :, 8:12], x[:, :, 1:2].broadcast_to([P, FH, 4]), y[:, :, 0:4], ALU.add)
                nc.vector.tensor_tensor(CD[:, :, 12:16].rearrange("p h (a b) -> p h a b", a=2),
                                        x[:, :, 2:4].unsqueeze(3).broadcast_to([P, FH, 2, 2]),
                                        y[:, :, 0:2].unsqueeze(2).broadcast_to([P, FH, 2, 2]), ALU.add)
                nc.vector.tensor_tensor(CD[:, :, 16:20], x[:, :, 4:8], y[:, :, 0:1].broadcast_to([P, FH, 4]), ALU.add).then_inc(S["cd"], 1)
            if part == 5:
                await_(dve, S["cd"], j + 1)
                for h in range(FH):
                    o = nc.vector.max(TOP[q][:, h, :], CD[:, h, :])
                o.then_inc(S["top"], 1)
                dve.wait_ge(S["top"], j + 1)
                nc.vector.tensor_tensor(D8[:, :, :], TOP[q][:, :, :], TOP[q][:, :, 0:1].broadcast_to([P, FH, TOPK]), ALU.subtract).then_inc(S["d8"], 1)
            if part == 6:
                dve.wait_ge(S["e8"], j + 1)
                nc.vector.tensor_reduce(Z[:, :], E8[:, :, :], AX.X, ALU.add).then_inc(S["z"], 1)
            if part == 7:
                dve.wait_ge(S["lz"], j + 1)
                nc.vector.scalar_tensor_tensor(out=NB[q][:, :], in0=LZ[:, :], scalar=-1.0, in1=TOP[q][:, :, 0], op0=ALU.mult, op1=ALU.subtract).then_inc(S["nb"], 1)

        dve.wait_ge(S["x2l"], 16)
        nc.vector.tensor_scalar(BNT[0][:, :], X2T[0][:, :], ab[:, 0:1], ab[:, 1:2], ALU.mult, ALU.add).then_inc(S["bnt"], 1)
        for part in range(8):
            choose(part, 0, 0, 0)

        def experts(j, g, b, k):
            dve.wait_ge(S["turned"], (j + 1) * FH)
            dve.wait_ge(S["ge"], (g + 1) * 2)
            wait_pos(dve, S["outp"], j - 1)
            nc.vector.tensor_tensor(CT[k % 2][:, :, :], WT[:, :, :], GE[b][:, :, k * P:(k + 1) * P], ALU.mult).then_inc(S["ct"], 1)

        def group(g, b, more):
            for k in range(GT):
                j = g * GT + k
                q = k % 2
                prev = (j - 1, g, b, k - 1) if k else (j - 1, g - 1, 1 - b, GT - 1)
                real = not (isinstance(j, int) and j == 0)
                for h in range(FH):
                    if more or k < GT - 1:
                        for part in PARTS[h]:
                            choose(part, j + 1, (k + 1) % 4, 1 - q)
                    if h == 1 and real:
                        experts(*prev)
                    dve.wait_ge(S["e"], j * FH + h + 1)
                    wait_pos(dve, S["turned"], j * FH + h - WRING + 1)
                    nc.vector.scalar_tensor_tensor(out=W[h % WRING][:, :], in0=SUM[(k * FH + h) % RING][:, :], scalar=TOP[q][:, h, TOPK - 1:TOPK],
                                                   in1=E[h % 2][:, :], op0=ALU.is_ge, op1=ALU.mult).then_inc(S["masked"], 1)

        steps(dve, group)
        experts(GROUPS * GT - 1, GROUPS - 1, 1, GT - 1)

    @block.tensor
    def _(pe):
        def similar(j, g, b, k, o_done):
            pe.wait_ge(S["bnt"], g + 1)
            wait_pos(pe, S["sim"], j)
            wait_pos(pe, S["o_r"], o_done)
            pe.matmul(MB[:, :], BNT[b][:, k * P:(k + 1) * P], KM[:, :], start=True, stop=True).then_inc(S["sim_p"], 1)

        def OB(g, k, more):
            return (g + 1) * BLK + (sum(1 for at in OSLOT if at < (k, SSLOT)) if more else 0)

        def o_block(g, b, e, sim_done):
            pe.wait_ge(S["x2l"], (g + 1) * 16)
            wait_pos(pe, S["o_r"], g * BLK + e)
            wait_pos(pe, S["sim"], sim_done)
            pe.matmul(MB[:, :], key_in[:, e * P:(e + 1) * P], X2T[b][:, :], start=True, stop=True).then_inc(S["o_p"], 1)

        for e in range(BLK):
            if e == SIM0:
                similar(0, 0, 0, 0, 0)
            pe.wait_ge(S["x2l"], 16)
            if e >= 4:
                pe.wait_ge(S["o_r"], e - 3)
            pe.matmul(E[e // 2 % 2][:, e % 2 * GN:(e % 2 + 1) * GN], key_in[:, e * P:(e + 1) * P], X2T[0][:, :],
                      start=True, stop=True).then_inc(S["o_p"], 1)
        similar(1, 0, 0, 1, 0)

        def outputs(j, g, b, k):
            po = POUT[:, :]
            pe.wait_ge(S["x1l"], (g + 1) * 16)
            wait_pos(pe, S["outs"], j)
            pe.matmul(po, ident[:, :], X1[b][:, k, :], start=True, stop=False)
            pe.wait_ge(S["ct"], j + 1)
            for e in range(BLK):
                o = pe.matmul(po, CT[k % 2][:, e, :], key_out[:, e, :], start=False, stop=(e == BLK - 1))
            o.then_inc(S["outp"], 1)

        def group(g, b, more):
            for k in range(GT):
                j = g * GT + k
                real = not (isinstance(j, int) and j == 0)
                for h in range(FH):
                    if h == SSLOT and (more or k < 2):
                        if k < 2:
                            similar(j + 2, g, b, k + 2, OB(g, k, more))
                        else:
                            similar(j + 2, g + 1, 1 - b, k - 2, OB(g, k, more))
                    if (k, h) in OSLOT and more:
                        o_block(g + 1, 1 - b, OSLOT.index((k, h)), j + 2 + (h >= SSLOT))
                    if h == 3 and real:
                        outputs(j - 1, *((g, b, k - 1) if k else (g - 1, 1 - b, GT - 1)))
                    pe.wait_ge(S["masked"], j * FH + h + 1)
                    if h == 0:
                        wait_pos(pe, S["ct"], j)
                    for e in range(BLK):
                        o = pe.matmul(WT[:, e, :], W[h % WRING][:, e * P:(e + 1) * P], ident[:, :], is_transpose=True,
                                      start=(h == 0 and e % 4 == 0), stop=(h == FH - 1), skip_group_check=True)
                    o.then_inc(S["turned"], 1)

        steps(pe, group)
        outputs(GROUPS * GT - 1, GROUPS - 1, 1, GT - 1)


def program(nc, x, w_qkvT, w_projT, ident, identb, band, w_q, keysT, key_inT, key_out, gb, out):
    x1 = nc.dram_tensor("x1", (SEQS * T, P), F32, kind="Internal").ap()
    x2T = nc.dram_tensor("x2T", (P, SEQS * T), F32, kind="Internal").ap()
    with ExitStack() as both:
        def sb(name, shape):
            return both.enter_context(nc.sbuf_tensor(name, shape, F32))

        idf = sb("idf", [P, P])
        KI = sb("KI", [P, NE])
        KO = sb("KO", [P, BLK, P])
        KM = sb("KM", [P, 2 * FH * NK])
        GB = sb("GB", [P, 2])
        bnst = sb("bnst", [P, SEQS, 6])
        extra = [(idf[:, :], ident), (KI[:, :], key_inT), (KO[:, :, :], key_out), (GB[:, :], gb)]
        with ExitStack() as ctx:
            attention(nc, ctx, x, w_qkvT, w_projT, identb, band, w_q, keysT, idf, bnst, KM, extra, x1, x2T)
        with ExitStack() as ctx:
            ffn(nc, ctx, x1, x2T, KM, KI, KO, GB, idf, bnst, out)


def kernel(L0_attn_x, L0_attn_w_qkv, L0_attn_w_proj, L0_ffn_gamma, L0_ffn_beta, L0_ffn_w_q, L0_ffn_keys,
           L0_ffn_key_in, L0_ffn_key_out):
    import ml_dtypes
    import numpy as np
    import concourse.bacc as bacc
    from concourse.bass_utils import run_bass_kernel_spmd

    w = np.asarray(L0_attn_w_qkv).reshape(3, P, P)
    dh = [w[n].reshape(H, DK, P).transpose(1, 0, 2).reshape(P, P) for n in range(2)]
    keep = np.arange(P)[None, :] >= np.arange(P)[:, None]
    arrays = {
        "x": np.asarray(L0_attn_x).reshape(SEQS * T, P),
        "w_qkvT": np.concatenate([dh[0].T, dh[1].T, w[2].T], axis=1),
        "w_projT": np.asarray(L0_attn_w_proj).T,
        "ident": np.eye(P, dtype=np.float32),
        "identb": np.eye(P, dtype=np.float32).astype(ml_dtypes.bfloat16),
        "band": np.concatenate([np.where(keep.T, 0, -1e30), np.where(keep, 0, -1e30)], axis=1).astype(ml_dtypes.bfloat16),
        "w_q": np.asarray(L0_ffn_w_q),
        "keysT": np.asarray(L0_ffn_keys).transpose(3, 2, 0, 1).reshape(P, 2 * FH * NK),
        "key_inT": np.asarray(L0_ffn_key_in).T,
        "key_out": np.asarray(L0_ffn_key_out).reshape(BLK, P, P).transpose(1, 0, 2),
        "gb": np.stack([np.asarray(L0_ffn_gamma), np.asarray(L0_ffn_beta)], axis=1),
    }
    arrays = {name: np.ascontiguousarray(a) for name, a in arrays.items()}
    nc = bacc.Bacc("TRN2", target_bir_lowering=False, num_devices=1)
    args = {name: nc.dram_tensor("in_" + name, a.shape, mybir.dt.from_np(a.dtype), kind="ExternalInput").ap()
            for name, a in arrays.items()}
    out = nc.dram_tensor("out_0", (SEQS * T, P), F32, kind="ExternalOutput").ap()
    program(nc, out=out, **args)
    ran = run_bass_kernel_spmd(nc, [{"in_" + name: a for name, a in arrays.items()}], core_ids=[0])
    return ran.results[0]["out_0"].reshape(SEQS, T, P)
```

```python
from contextlib import ExitStack

import numpy as np
import concourse.bass as bass
from concourse import mybir

F32 = mybir.dt.float32
BF16 = mybir.dt.bfloat16
ACT = mybir.ActivationFunctionType
ALU = mybir.AluOpType
AX = mybir.AxisListType

P = 128
SEQS = 16
T = 512
TILES = T // P
H = 16
DK = P // H
EPS = 1e-5
TERMS = 9
KQ = TERMS * DK
SHIFT = 3
TWO_ONES = float(np.array([0x3F803F80], np.uint32).view(np.float32)[0])
SLOT_V = 32
SLOT_PT = 1280
VSLOT = ((6, 1), (10, 1), (14, 1), (2, 2))
ASLOT = (3, 7, 8, 10)


def attention(nc, ctx, x, w_qkvT, w_projT, identb, band, w_q, keysT, idf, bnst, KM, extra, x1_out, x2T_out):
    def sb(name, shape, dt=F32):
        return ctx.enter_context(nc.sbuf_tensor(name, shape, dt))

    def ps(name, shape, dt=F32):
        return ctx.enter_context(nc.psum_tensor(name, shape, dt))

    def sem(name):
        return ctx.enter_context(nc.semaphore(name))

    xs = x.rearrange("(s i p) c -> s p i c", i=TILES, p=P)
    x1s = x1_out.rearrange("(s i p) c -> s p i c", i=TILES, p=P)
    x2Ts = x2T_out.rearrange("c (s n) -> s c n", n=T)
    q_parts = nc.dram_tensor("q_parts", (3, P, T), BF16, kind="Internal").ap()
    k_parts = nc.dram_tensor("k_parts", (3, P, T), BF16, kind="Internal").ap()

    m_parts = nc.dram_tensor("m_parts", (3, H, T), BF16, kind="Internal").ap()

    wq = sb("wq", [P, 3 * P])
    wp = sb("wp", [P, P])
    WQF = sb("WQF", [P, 2 * FH, P])
    KT = sb("KT", [P, 2 * FH * NK])
    idb = sb("idb", [P, P], BF16)
    bandb = sb("bandb", [P, 2 * P], BF16)
    xin = [sb(f"xin{b}", [P, TILES, P]) for b in range(2)]
    xres = sb("xres", [P, TILES, P])
    st6 = sb("st6", [P, TILES, 6])
    mv = sb("mv", [P, TILES, 2])
    ve = sb("ve", [P, TILES])
    half = sb("half", [P, TILES])
    rs = sb("rs", [P, TILES])
    xn = sb("xn", [P, TILES, P])
    xnT = [sb(f"xnT{b}", [P, T]) for b in range(2)]
    qp = sb("qp", [P, 3, T], BF16)
    kp = sb("kp", [P, 3, T], BF16)
    rq = sb("rq", [P, T])
    rk = sb("rk", [P, T])
    Q = [sb(f"Q{b}", [P, H, T], BF16) for b in range(2)]
    K = [sb(f"K{b}", [P, H, T], BF16) for b in range(2)]
    V = [sb(f"V{b}", [P, TILES, H, SLOT_V]) for b in range(2)]
    mx = sb("mx", [P, H, TILES])
    mp = sb("mp", [H // 2, 3, T], BF16)
    rm = sb("rm", [H // 2, T])
    PT = sb("PT", [P, 8, SLOT_PT])
    U = [sb(f"U{b}", [P, 4, T]) for b in range(2)]
    rec = sb("rec", [P, TILES, H])
    A = sb("A", [P, TILES, P])
    AT = sb("AT", [P, T])
    X1 = sb("X1", [P, TILES, P])
    t6 = sb("t6", [P, TILES, 6])
    tv = sb("tv", [P, TILES, 2])
    te = sb("te", [P, TILES])
    trs = sb("trs", [P, TILES])
    X2 = sb("X2", [P, TILES, P])
    X2T = sb("X2T", [P, T])

    SX = ps("SX", [P, 2, 256])
    SY = ps("SY", [P, 2, 512])
    TX = ps("TX", [P, 2, 256])
    TY = ps("TY", [P, 2, 512])
    PV = ps("PV", [P, T])
    MB = ps("MB", [P, TILES, P])

    names = ("waits_passed max_parts_stored memory_loaded keys_merged keys_copied consts_loaded "
             "v_pads_set k_ones_set x_variance x_rstd x_loaded xn_ready xn_turned xnT_ready q_product "
             "q_part1 q_rest q_part2 q_part3 k_product k_part1 k_rest k_part2 k_part3 v_product "
             "v_ready q_stored k_stored heads_0_7_loaded heads_8_15_loaded outer_scores inner_scores "
             "outer_maxima inner_maxima outer_scoresT inner_scoresT outer_exp inner_exp exp_masked "
             "values_product values_copied maxima_turned max_part1 max_rest max_part2 max_part3 "
             "max_rows_loaded att_turned att_normed attT_product attT_copied projected x1_ready "
             "x1_variance x1_rstd x2_ready x2_turned x2T_ready bn_stats_ready residual_loaded "
             "x1_stored x2T_stored x_stats x_means sums_inverted x1_stats x1_means").split()
    S = {n: sem("a_" + n) for n in names}

    def steps(eng, do):
        for t in (-1, 0, 1):
            do(t, t)
        with eng.Fori(0, 6) as i:
            do(i * 2 + 2, 2)
            do(i * 2 + 3, 3)
        for t in (14, 15, 16, 17):
            do(t, t)

    SHARED = [(1, "mt1", -1, "max_rest", 2, 2), (3, "att0", -2, "att_normed", 4, 1), (4, "xnT", 1, "xnT_ready", 1, 1),
              (5, "q", 1, "q_rest", 1, 1), (6, "k", 1, "k_rest", 1, 1), (7, "att1", -2, "att_normed", 4, 2), (8, "att2", -2, "att_normed", 4, 3),
              (9, "mt0", 0, "max_rest", 2, 1), (10, "att3", -2, "att_normed", 4, 4), (11, "at", -2, "attT_copied", 1, 1),
              (12, "pj", -2, "x1_ready", 1, 1), (13, "v", 0, "v_ready", 1, 1), (15, "x2T", -2, "x2T_ready", 1, 1)]
    ORDER = [n for _, n, *_ in SHARED]

    def bank_free(pe, name, t, c):
        at = ORDER.index(name)
        for back in range(1, len(SHARED) + 1):
            j, dt = (at - back) % len(SHARED), -1 if back > at else 0
            _, _, off, sname, per, nth = SHARED[j]
            if 0 <= c + dt + off < SEQS:
                pe.wait_ge(S[sname], (t + dt + off) * per + nth)
                return

    def await_(eng, semaphore, count):
        eng.wait_ge(semaphore, count)
        eng.sem_inc(S["waits_passed"], 1)

    block = ctx.enter_context(nc.Block())

    @block.sync
    def _(sp):
        sp.dma_start(xin[0][:, :, :], xs[0]).then_inc(S["x_loaded"], 16)
        for dst, src in ((wq[:, :], w_qkvT), (wp[:, :], w_projT), (idb[:, :], identb), (bandb[:, :], band)):
            sp.dma_start(dst, src).then_inc(S["consts_loaded"], 16)
        for dst, src in extra[:1]:
            sp.dma_start(dst, src).then_inc(S["consts_loaded"], 16)
        sp.wait_ge(S["x_loaded"], 16)
        sp.dma_start(xin[1][:, :, :], xs[1]).then_inc(S["x_loaded"], 16)
        sp.wait_ge(S["x_loaded"], 32)
        for dst, src in [(WQF[:, :, :], w_q.rearrange("(g k) d -> k g d", k=P)), (KT[:, :], keysT)] + extra[1:]:
            sp.dma_start(dst, src).then_inc(S["memory_loaded"], 16)

        def back(t, half_, b):
            hs = slice(8 * half_, 8 * half_ + 8)
            to = S["heads_0_7_loaded"] if half_ == 0 else S["heads_8_15_loaded"]
            for a in range(3):
                sp.dma_start(K[b][24 * a:24 * a + 24, hs, :],
                             k_parts.rearrange("a (d h) n -> (a d) h n", h=H)[:, hs, :]).then_inc(to, 16)
                for e in range(3):
                    r = 24 * a + 8 * e
                    sp.dma_start(Q[b][r:r + 8, hs, :],
                                 q_parts[a].rearrange("(d h) n -> d h n", h=H)[:, hs, :]).then_inc(to, 16)

        def shift_rows(t, half_, b):
            hs = slice(8 * half_, 8 * half_ + 8)
            sp.dma_start(m_parts[:, hs, :].rearrange("r h n -> h r n"), mp[:, :, :]).then_inc(S["max_parts_stored"], 16)
            await_(sp, S["max_parts_stored"], 16 * (2 * t + half_ + 1))
            sp.dma_start(Q[b][KQ:KQ + 3, hs, :], m_parts[:, hs, :]).then_inc(S["max_rows_loaded"], 16)

        def step(t, c):
            if 0 <= c - 2 < SEQS:
                if c - 3 >= 0:
                    await_(sp, S["x1_ready"], t - 2)
                sp.dma_start(xres[:, :, :], xs[t - 2]).then_inc(S["residual_loaded"], 16)
            if 0 <= c - 1 < SEQS:
                await_(sp, S["max_part3"], (t - 1) * 2 + 2)
                shift_rows(t - 1, 1, (c - 1) % 2)
            if 0 <= c + 1 < SEQS:
                await_(sp, S["q_part3"], t + 2)
                if c >= 0:
                    await_(sp, S["heads_0_7_loaded"], 16 * 12 * (t + 1))
                    await_(sp, S["heads_8_15_loaded"], 16 * 12 * (t + 1))
                sp.dma_start(q_parts.rearrange("a p n -> p a n"), qp[:, :, :]).then_inc(S["q_stored"], 16)
                await_(sp, S["k_part3"], t + 2)
                sp.dma_start(k_parts.rearrange("a p n -> p a n"), kp[:, :, :]).then_inc(S["k_stored"], 16)
                await_(sp, S["q_stored"], 16 * (t + 2))
                await_(sp, S["k_stored"], 16 * (t + 2))
                if c - 1 >= 0:
                    await_(sp, S["inner_scoresT"], (t - 1) * H + 8)
                if c >= 0 and c + 2 < SEQS:
                    sp.dma_start(xin[c % 2][:, :, :], xs[t + 2]).then_inc(S["x_loaded"], 16)
                if c <= 0:
                    sp.wait_ge(S["k_ones_set"], c + 2)
                back(t + 1, 0, (c + 1) % 2)
            if 0 <= c < SEQS:
                await_(sp, S["max_part3"], t * 2 + 1)
                shift_rows(t, 0, c % 2)
            if 0 <= c - 2 < SEQS:
                await_(sp, S["x1_ready"], t - 1)
                sp.dma_start(x1s[t - 2], X1[:, :, :]).then_inc(S["x1_stored"], 16)
                await_(sp, S["x2T_ready"], t - 1)
                sp.dma_start(x2Ts[t - 2], X2T[:, :]).then_inc(S["x2T_stored"], 16)
            if 0 <= c + 1 < SEQS:
                if c - 1 >= 0:
                    await_(sp, S["inner_scoresT"], (t - 1) * H + 16)
                back(t + 1, 1, (c + 1) % 2)

        steps(sp, step)
        await_(sp, S["x1_stored"], 16 * SEQS)
        await_(sp, S["x2T_stored"], 16 * SEQS)

    @block.gpsimd
    def _(pool):
        nc.gpsimd.memset(half[:, :], -0.5).then_inc(S["v_pads_set"], 1)
        for b in range(2):
            nc.gpsimd.memset(V[b][:, :, :, :], 0.0).then_inc(S["v_pads_set"], 1)
        pool.wait_ge(S["v_pads_set"], 3)
        for b in range(2):
            nc.gpsimd.memset(V[b][:, :, :, DK:DK + 1], 1.0).then_inc(S["v_pads_set"], 1)

        def mask(out, pairs, stop_low):
            s = 1 if stop_low else -1
            return nc.gpsimd.affine_select(out=out, in_=out, compare_op=ALU.is_ge, fill=0.0, base=0,
                                           pattern=([[0, 2]] if pairs else []) + [[s, P]], channel_multiplier=-s)

        def step(t, c):
            for h in range(H):
                if h == 1 and 0 <= c + 1 < SEQS:
                    pool.wait_ge(S["x_variance"], t + 2)
                    nc.gpsimd.tensor_tensor(rs[:, :], ve[:, :], half[:, :], ALU.pow).then_inc(S["x_rstd"], 1)
                if 0 <= c - 1 < SEQS:
                    pt = PT[:, h % 8, :]
                    y = pt[:, 512:1280].rearrange("p (j n) -> p j n", j=2)
                    await_(pool, S["outer_exp"], (t - 1) * H + h + 1)
                    mask(pt[:, 128:256], False, False).then_inc(S["exp_masked"], 1)
                    mask(pt[:, 256:384], False, True).then_inc(S["exp_masked"], 1)
                    await_(pool, S["inner_exp"], (t - 1) * H + h + 1)
                    mask(y[:, :, 0:128], True, True).then_inc(S["exp_masked"], 1)
                    mask(y[:, :, 256:384], True, False).then_inc(S["exp_masked"], 1)
                if h == 13 and 0 <= c - 2 < SEQS:
                    pool.wait_ge(S["x1_variance"], t - 1)
                    nc.gpsimd.tensor_tensor(trs[:, :], te[:, :], half[:, :], ALU.pow).then_inc(S["x1_rstd"], 1)

        steps(pool, step)

    @block.scalar
    def _(act):
        act.wait_ge(S["v_pads_set"], 5)

        def step(t, c):
            b = c % 2
            for h in range(H):
                if h == 1 and 0 <= c - 1 < SEQS:
                    shift(t - 1, 2)
                if h == 9 and 0 <= c < SEQS:
                    shift(t, 1)
                if h == 4 and 0 <= c + 1 < SEQS:
                    act.wait_ge(S["xn_turned"], t + 2)
                    if c - 1 >= 0:
                        act.wait_ge(S["v_product"], t)
                    nc.scalar.copy(xnT[1 - b][:, :].rearrange("p (i n) -> p i n", n=P), MB[:, :, :]).then_inc(S["xnT_ready"], 1)
                for hh, nm, src, dst, r, sc in ((5, "q", MB, qp, rq, DK ** -0.5), (6, "k", MB, kp, rk, 1.0)):
                    if h == hh and 0 <= c + 1 < SEQS:
                        act.wait_ge(S[nm + "_product"], t + 2)
                        if c >= 0:
                            act.wait_ge(S[nm + "_stored"], 16 * (t + 1))
                        nc.scalar.mul(dst[:, 0, :].rearrange("p (i n) -> p i n", n=P), src[:, :, :], sc).then_inc(S[nm + "_part1"], 1)
                    if h == hh + 1 and 0 <= c + 1 < SEQS:
                        act.wait_ge(S[nm + "_rest"], t + 2)
                        nc.scalar.copy(dst[:, 1, :], r[:, :]).then_inc(S[nm + "_part2"], 1)
                if h == 8 and c == -1:
                    act.wait_ge(S["keys_merged"], 1)
                    nc.scalar.copy(KM[:, :], MB[:, :, :].rearrange("p i n -> p (i n)")).then_inc(S["keys_copied"], 1)
                if h == 13 and 0 <= c < SEQS:
                    act.wait_ge(S["v_product"], t + 1)
                    if c >= 2:
                        act.wait_ge(S["values_product"], (t - 1) * 4)
                    nc.scalar.copy(V[b][:, :, :, 0:DK], MB[:, :, :].rearrange("p i (h d) -> p i h d", d=DK)).then_inc(S["v_ready"], 1)
                for g, (sl, ds_) in enumerate(VSLOT):
                    if h == sl and 0 <= c - ds_ < SEQS:
                        act.wait_ge(S["values_product"], (t - ds_) * 4 + g + 1)
                        if c - ds_ >= 2:
                            act.wait_ge(S["att_turned"], (t - ds_ - 1) * 4)
                        nc.scalar.copy(U[(c - ds_) % 2][:, g, :], PV[:, :]).then_inc(S["values_copied"], 1)
                if h == 11 and 0 <= c - 2 < SEQS:
                    act.wait_ge(S["attT_product"], t - 1)
                    nc.scalar.copy(AT[:, :].rearrange("p (i n) -> p i n", n=P), MB[:, :, :]).then_inc(S["attT_copied"], 1)
                if h == 15 and 0 <= c - 2 < SEQS:
                    act.wait_ge(S["x2_turned"], t - 1)
                    if c - 2 >= 1:
                        act.wait_ge(S["x2T_stored"], 16 * (t - 2))
                        act.wait_ge(S["bn_stats_ready"], t - 2)
                    nc.scalar.copy(X2T[:, :].rearrange("p (i n) -> p i n", n=P), MB[:, :, :]).then_inc(S["x2T_ready"], 1)
                if 0 <= c - 1 < SEQS:
                    pt = PT[:, h % 8, :]
                    n = (t - 1) * H + h + 1
                    act.wait_ge(S["outer_scoresT"], n)
                    if h >= 8:
                        act.wait_ge(S["values_product"], (t - 1) * 4 + (h - 8) // 4 + 1)
                    elif c - 1 >= 1:
                        act.wait_ge(S["values_product"], (t - 2) * 4 + 2 + h // 4 + 1)
                    nc.scalar.activation(pt[:, 0:512], TX[:, :, :].rearrange("p j n -> p (j n)"), ACT.Exp).then_inc(S["outer_exp"], 1)
                    act.wait_ge(S["inner_scoresT"], n)
                    nc.scalar.activation(pt[:, 512:1280].rearrange("p (j n) -> p j n", j=2), TY[:, :, 0:384], ACT.Exp).then_inc(S["inner_exp"], 1)

        def shift(s, nth):
            act.wait_ge(S["maxima_turned"], s * 2 + nth)
            prev = (s * 2 + nth - 1)
            if not isinstance(prev, int) or prev >= 1:
                act.wait_ge(S["max_rows_loaded"], prev * 16)
            nc.scalar.mul(mp[:, 0, :].rearrange("p (i n) -> p i n", n=P), MB[0:8, :, :], -1.0).then_inc(S["max_part1"], 1)
            act.wait_ge(S["max_rest"], s * 2 + nth)
            nc.scalar.copy(mp[:, 1, :], rm[:, :]).then_inc(S["max_part2"], 1)

        steps(act, step)

    @block.vector
    def _(dve):

        def stats(part, s, src, a6, av, ae, s1, s2, to):
            if part == 0:
                for i in range(TILES):
                    nc.vector.bn_stats(a6[:, i, :], src[:, i, :]).then_inc(s1, 1)
                return
            await_(dve, s1, (s + 1) * TILES)
            for i in range(TILES):
                nc.vector.bn_aggr(av[:, i, :], a6[:, i, :]).then_inc(s2, 1)
            dve.wait_ge(s2, (s + 1) * TILES)
            nc.vector.tensor_scalar(ae[:, :], av[:, :, 1], EPS, None, ALU.add).then_inc(to, 1)

        def norm(src, av, r, dst, to):
            for i in range(TILES):
                o = nc.vector.tensor_scalar(dst[:, i, :], src[:, i, :], av[:, i, 0:1], r[:, i:i + 1], ALU.subtract, ALU.mult)
            o.then_inc(to, 1)

        def shift(s, nth):
            dve.wait_ge(S["max_part1"], s * 2 + nth)
            nc.vector.scalar_tensor_tensor(out=rm[:, :].rearrange("p (i n) -> p i n", n=P), in0=MB[0:8, :, :], scalar=-1.0,
                                           in1=mp[:, 0, :].rearrange("p (i n) -> p i n", n=P), op0=ALU.mult, op1=ALU.subtract).then_inc(S["max_rest"], 1)
            dve.wait_ge(S["max_part2"], s * 2 + nth)
            nc.vector.tensor_tensor(mp[:, 2, :], rm[:, :], mp[:, 1, :], ALU.subtract).then_inc(S["max_part3"], 1)

        def step(t, c):
            b = c % 2
            for h in range(H):
                if 0 <= c < SEQS:
                    n = t * H + h + 1
                    dve.wait_ge(S["outer_scores"], n)
                    if h == 0 and c >= 1:
                        dve.wait_ge(S["maxima_turned"], t * 2 - 1)
                    if h == 8 and c >= 1:
                        dve.wait_ge(S["maxima_turned"], t * 2)
                    nc.vector.tensor_reduce(mx[:, h, 0:4:3], SX[:, :, :], AX.X, ALU.max).then_inc(S["outer_maxima"], 1)
                    dve.wait_ge(S["inner_scores"], n)
                    nc.vector.tensor_reduce(mx[:, h, 1:3], SY[:, :, 0:384], AX.X, ALU.max).then_inc(S["inner_maxima"], 1)
                if h == 1 and 0 <= c - 1 < SEQS:
                    shift(t - 1, 2)
                if h == 9 and 0 <= c < SEQS:
                    shift(t, 1)
                if h == 0 and 0 <= c + 1 < SEQS:
                    dve.wait_ge(S["x_loaded"], 16 * (t + 2))
                    stats(0, t + 1, xin[1 - b], st6, mv, ve, S["x_stats"], S["x_means"], S["x_variance"])
                if h == 1 and 0 <= c + 1 < SEQS:
                    stats(1, t + 1, xin[1 - b], st6, mv, ve, S["x_stats"], S["x_means"], S["x_variance"])
                if h == 3 and 0 <= c + 1 < SEQS:
                    dve.wait_ge(S["x_rstd"], t + 2)
                    if c >= 0:
                        dve.wait_ge(S["xn_turned"], t + 1)
                    norm(xin[1 - b], mv, rs, xn, S["xn_ready"])
                if c == -1 and h in (4, 7):
                    both = K[0 if h == 4 else 1][64:P, :, :].rearrange("p h n -> p (h n)").bitcast(F32)
                    nc.vector.memset(both, TWO_ONES).then_inc(S["k_ones_set"], 1)
                for hh, nm, dst, r, sc in ((5, "q", qp, rq, DK ** -0.5), (6, "k", kp, rk, 1.0)):
                    if h == hh and 0 <= c + 1 < SEQS:
                        dve.wait_ge(S[nm + "_part1"], t + 2)
                        nc.vector.scalar_tensor_tensor(out=r[:, :].rearrange("p (i n) -> p i n", n=P), in0=MB[:, :, :], scalar=sc,
                                                       in1=dst[:, 0, :].rearrange("p (i n) -> p i n", n=P),
                                                       op0=ALU.mult, op1=ALU.subtract).then_inc(S[nm + "_rest"], 1)
                    if h == hh + 1 and 0 <= c + 1 < SEQS:
                        dve.wait_ge(S[nm + "_part2"], t + 2)
                        nc.vector.tensor_tensor(dst[:, 2, :], r[:, :], dst[:, 1, :], ALU.subtract).then_inc(S[nm + "_part3"], 1)
                for i, sl in enumerate(ASLOT):
                    if h == sl and 0 <= c - 2 < SEQS:
                        n = (t - 2) * 4 + i + 1
                        dve.wait_ge(S["att_turned"], n)
                        hv = MB[:, :, :].rearrange("p g (h e) -> p (g h) e", e=SLOT_V)
                        nc.vector.reciprocal(rec[:, i, :], hv[:, :, DK]).then_inc(S["sums_inverted"], 1)
                        dve.wait_ge(S["sums_inverted"], n)
                        nc.vector.tensor_tensor(A[:, i, :].rearrange("p (h d) -> p h d", d=DK), hv[:, :, 0:DK],
                                                rec[:, i, :].unsqueeze(2).broadcast_to([P, H, DK]), ALU.mult).then_inc(S["att_normed"], 1)
                if h == 12 and 0 <= c - 2 < SEQS:
                    dve.wait_ge(S["projected"], t - 1)
                    dve.wait_ge(S["residual_loaded"], 16 * (t - 1))
                    if c - 2 >= 1:
                        dve.wait_ge(S["x1_stored"], 16 * (t - 2))
                    nc.vector.tensor_tensor(X1[:, :, :], MB[:, :, :], xres[:, :, :], ALU.add).then_inc(S["x1_ready"], 1)
                if h == 13 and 0 <= c - 2 < SEQS:
                    dve.wait_ge(S["x1_ready"], t - 1)
                    stats(0, t - 2, X1, t6, tv, te, S["x1_stats"], S["x1_means"], S["x1_variance"])
                    stats(1, t - 2, X1, t6, tv, te, S["x1_stats"], S["x1_means"], S["x1_variance"])
                if h == 14 and 0 <= c - 2 < SEQS:
                    dve.wait_ge(S["x1_rstd"], t - 1)
                    norm(X1, tv, trs, X2, S["x2_ready"])
            if 0 <= c - 2 < SEQS:
                dve.wait_ge(S["x2T_ready"], t - 1)
                nc.vector.bn_stats(bnst[:, t - 2, :] if isinstance(t, int) else bnst[:, bass.ds(t - 2, 1), :].rearrange("p o n -> p (o n)"), X2T[:, :]).then_inc(S["bn_stats_ready"], 1)

        steps(dve, step)

    @block.tensor
    def _(pe):
        pe.wait_ge(S["consts_loaded"], 80)
        pe.wait_ge(S["v_pads_set"], 5)
        HI, LO = bandb[:, 0:P], bandb[:, P:2 * P]

        def scores(t, c, h):
            b, n = c % 2, t * H + h + 1
            if h == 0:
                pe.wait_ge(S["heads_0_7_loaded"], 192 * (t + 1))
            if h == 8:
                pe.wait_ge(S["heads_8_15_loaded"], 192 * (t + 1))

            def tile(out, i, k0, k1, clear=True):
                pe.matmul(out, Q[b][0:KQ, h, i * P:(i + 1) * P], K[b][0:KQ, h, k0 * P:k1 * P],
                          start=clear, stop=False, skip_group_check=True)

            def outside(out, band_):
                return pe.matmul(out, idb[:, :], band_, start=False, stop=True, skip_group_check=True)

            if c > 0 or h > 0:
                pe.wait_ge(S["outer_maxima"], n - 1)
            tile(SX[:, 0, :], 0, 0, 2)
            tile(SX[:, 1, :], 3, 2, 4, False)
            outside(SX[:, :, :].rearrange("p j n -> p (j n)")[:, P:3 * P], bandb[:, :]).then_inc(S["outer_scores"], 1)
            if c > 0 or h > 0:
                pe.wait_ge(S["inner_maxima"], n - 1)
            for n, i in enumerate((1, 2)):
                tile(SY[:, n, 0:3 * P], i, i - 1, i + 2)
                outside(SY[:, n, 0:P], LO)
                o = outside(SY[:, n, 2 * P:3 * P], HI)
            o.then_inc(S["inner_scores"], 1)

        def scoresT(t, c, h):
            s = t - 1
            b, n = (c - 1) % 2, s * H + h + 1
            R = KQ + SHIFT
            if h == 0:
                pe.wait_ge(S["max_rows_loaded"], 32 * s + 16)
            if h == 8:
                pe.wait_ge(S["max_rows_loaded"], 32 * s + 32)

            def tile(out, j, q0, q1):
                return pe.matmul(out[:, 0:(q1 - q0) * P], K[b][0:R, h, j * P:(j + 1) * P], Q[b][0:R, h, q0 * P:q1 * P],
                                 start=True, stop=True, skip_group_check=True)

            if c > 1 or h > 0:
                pe.wait_ge(S["outer_exp"], n - 1)
            tile(TX[:, 0, :], 0, 0, 2)
            tile(TX[:, 1, :], 3, 2, 4).then_inc(S["outer_scoresT"], 1)
            if c > 1 or h > 0:
                pe.wait_ge(S["inner_exp"], n - 1)
            tile(TY[:, 0, :], 1, 0, 3)
            tile(TY[:, 1, :], 2, 1, 4).then_inc(S["inner_scoresT"], 1)

        SPAN = [(0, 0, 2), (512, 0, 3), (896, 1, 4), (256, 2, 4)]

        def values(s, c, g):
            b = c % 2
            pe.wait_ge(S["exp_masked"], (s * H + 4 * g + 4) * 4)
            if g == 0:
                pe.wait_ge(S["v_ready"], s + 1)
            if c > 0 or g > 0:
                pe.wait_ge(S["values_copied"], s * 4 + g)
            for j, (at, q0, q1) in enumerate(SPAN):
                for e in range(4):
                    h = 4 * g + e
                    o = pe.matmul(PV[32 * e:32 * e + 32, q0 * P:q1 * P], V[b][:, j, h, :],
                                  PT[:, h % 8, at:at + (q1 - q0) * P], start=(j == 0), stop=(j == 3), skip_group_check=True)
            o.then_inc(S["values_product"], 1)

        def step(t, c):
            b = c % 2
            for h in range(H):
                if 0 <= c < SEQS:
                    scores(t, c, h)
                if h == 1 and 0 <= c - 1 < SEQS:
                    bank_free(pe, "mt1", t, c)
                    pe.wait_ge(S["inner_maxima"], t * H)
                    for i in range(TILES):
                        o = pe.transpose(MB[0:8, i, :], mx[:, 8:16, i], idf[:, :])
                    o.then_inc(S["maxima_turned"], 1)
                if h == 9 and 0 <= c < SEQS:
                    bank_free(pe, "mt0", t, c)
                    pe.wait_ge(S["inner_maxima"], t * H + 8)
                    for i in range(TILES):
                        o = pe.transpose(MB[0:8, i, :], mx[:, 0:8, i], idf[:, :])
                    o.then_inc(S["maxima_turned"], 1)
                if h == 4 and 0 <= c + 1 < SEQS:
                    bank_free(pe, "xnT", t, c)
                    pe.wait_ge(S["xn_ready"], t + 2)
                    for i in range(TILES):
                        o = pe.transpose(MB[:, i, :], xn[:, i, :], idf[:, :])
                    o.then_inc(S["xn_turned"], 1)
                if h == 5 and 0 <= c + 1 < SEQS:
                    bank_free(pe, "q", t, c)
                    pe.wait_ge(S["xnT_ready"], t + 2)
                    pe.matmul(MB[:, :, :], wq[:, 0:P], xnT[1 - b][:, :], start=True, stop=True).then_inc(S["q_product"], 1)
                if h == 6 and 0 <= c + 1 < SEQS:
                    bank_free(pe, "k", t, c)
                    pe.matmul(MB[:, :, :], wq[:, P:2 * P], xnT[1 - b][:, :], start=True, stop=True).then_inc(S["k_product"], 1)
                if h == 8 and c == -1:
                    pe.wait_ge(S["memory_loaded"], 16 * (2 + len(extra) - 1))
                    pe.wait_ge(S["k_rest"], 1)
                    mb = MB[:, :, :].rearrange("p i n -> p (i n)")
                    for g in range(2 * FH):
                        o = pe.matmul(mb[:, g * NK:(g + 1) * NK], WQF[:, g, :], KT[:, g * NK:(g + 1) * NK], start=True, stop=True)
                    o.then_inc(S["keys_merged"], 1)
                    pe.wait_ge(S["keys_copied"], 1)
                if h == 13 and 0 <= c < SEQS:
                    bank_free(pe, "v", t, c)
                    for i in range(TILES):
                        o = pe.matmul(MB[:, i, :], xnT[b][:, i * P:(i + 1) * P], wq[:, 2 * P:3 * P], start=True, stop=True)
                    o.then_inc(S["v_product"], 1)
                for i, sl in enumerate(ASLOT):
                    if h == sl and 0 <= c - 2 < SEQS:
                        bank_free(pe, f"att{i}", t, c)
                        pe.wait_ge(S["values_copied"], (t - 1) * 4)
                        for g in range(4):
                            o = pe.transpose(MB[:, g, :], U[b][:, g, i * P:(i + 1) * P], idf[:, :])
                        o.then_inc(S["att_turned"], 1)
                if h == 11 and 0 <= c - 2 < SEQS:
                    bank_free(pe, "at", t, c)
                    for i in range(TILES):
                        o = pe.transpose(MB[:, i, :], A[:, i, :], idf[:, :])
                    o.then_inc(S["attT_product"], 1)
                if h == 12 and 0 <= c - 2 < SEQS:
                    bank_free(pe, "pj", t, c)
                    for i in range(TILES):
                        o = pe.matmul(MB[:, i, :], AT[:, i * P:(i + 1) * P], wp[:, :], start=True, stop=True)
                    o.then_inc(S["projected"], 1)
                if h == 15 and 0 <= c - 2 < SEQS:
                    bank_free(pe, "x2T", t, c)
                    pe.wait_ge(S["x2_ready"], t - 1)
                    for i in range(TILES):
                        o = pe.transpose(MB[:, i, :], X2[:, i, :], idf[:, :])
                    o.then_inc(S["x2_turned"], 1)
                for g, (sl, ds_) in enumerate(VSLOT):
                    if h == sl and 0 <= c - ds_ < SEQS:
                        values(t - ds_, c - ds_, g)
                if 0 <= c - 1 < SEQS:
                    scoresT(t, c, h)

        steps(pe, step)


GROUPS = 16
GT = 4
GN = GT * P
FH = 8
NK = 32
NE = NK * NK
BLK = NE // P
TOPK = 8
CAND = 20
RING = 16
WRING = 8
PARTS = ((0, 1), (2,), (3,), (4, 5), (), (6,), (7,), ())
OSLOT = [(0, 5), (0, 7), (1, 2), (1, 5), (1, 7), (2, 2), (2, 5), (2, 7)]
SIM0 = 3
SSLOT = 4
GSLOT = [(2, 2), (3, 2)]
LEAD = 3


def ffn(nc, ctx, x1, x2T, KM, key_in, key_out, gb, ident, bnst, out):
    def sb(name, shape, dt=F32):
        return ctx.enter_context(nc.sbuf_tensor(name, shape, dt))

    def ps(name, shape, dt=F32):
        return ctx.enter_context(nc.psum_tensor(name, shape, dt))

    def sem(name):
        return ctx.enter_context(nc.semaphore(name))

    x1g = x1.rearrange("(g i p) c -> g p i c", i=GT, p=P)
    outg = out.rearrange("(g i p) c -> g p i c", i=GT, p=P)
    x2Tg = x2T.rearrange("c (g n) -> g c n", n=GN)

    mvb = sb("mvb", [P, 2])
    vb = sb("vb", [P, 1])
    hb = sb("hb", [P, 1])
    rb = sb("rb", [P, 1])
    ab = sb("ab", [P, 2])
    X2T = [sb(f"X2T{b}", [P, GN]) for b in range(2)]
    X1 = [sb(f"X1{b}", [P, GT, P]) for b in range(2)]
    BNT = [sb(f"BNT{b}", [P, GN]) for b in range(2)]
    GE = [sb(f"GE{b}", [P, BLK, GN]) for b in range(2)]
    OUT = [sb(f"OUT{b}", [P, GT, P]) for b in range(2)]
    SIM = [sb(f"SIM{b}", [P, 2, FH, NK]) for b in range(4)]
    M8 = [sb(f"M8{b}", [P, 2, FH, TOPK]) for b in range(2)]
    CD = sb("CD", [P, FH, CAND])
    TOP = [sb(f"TOP{b}", [P, FH, TOPK]) for b in range(2)]
    D8 = sb("D8", [P, FH, TOPK])
    E8 = sb("E8", [P, FH, TOPK])
    Z = sb("Z", [P, FH])
    LZ = sb("LZ", [P, FH])
    NB = [sb(f"NB{b}", [P, FH]) for b in range(2)]
    SUM = [sb(f"SUM{b}", [P, NE]) for b in range(RING)]
    W = [sb(f"W{b}", [P, NE]) for b in range(WRING)]
    CT = [sb(f"CT{b}", [P, BLK, P]) for b in range(2)]

    E = [ps(f"E{b}", [P, NE]) for b in range(2)]
    WT = ps("WT", [P, BLK, P])
    MB = ps("MB2", [P, GN])
    POUT = ps("POUT", [P, P])

    names = ("waits_passed half_set bn_mean bn_variance bn_rstd bn_coef x1_loaded x2T_loaded bn_rows "
             "sim_product sim_copied pair_sums exp_ready weights_masked weights_turned "
             "experts_weighted out_product out_copied expert_product expert_copied gelu_ready "
             "out_stored ranked candidates top_ready top_less_max top_exp exp_sum log_sum bias_ready").split()
    S = {n: sem("f_" + n) for n in names}

    def steps(eng, do):
        do(0, 0, True)
        do(1, 1, True)
        with eng.Fori(1, GROUPS // 2 - 1) as i:
            do(i * 2, 0, True)
            do(i * 2 + 1, 1, True)
        do(GROUPS - 2, 0, True)
        do(GROUPS - 1, 1, False)

    def wait_pos(eng, s, v):
        if not isinstance(v, int) or v > 0:
            eng.wait_ge(s, v)

    def await_(eng, semaphore, count):
        eng.wait_ge(semaphore, count)
        eng.sem_inc(S["waits_passed"], 1)

    block = ctx.enter_context(nc.Block())

    @block.sync
    def _(sp):
        sp.dma_start(X2T[0][:, :], x2Tg[0]).then_inc(S["x2T_loaded"], 16)
        sp.dma_start(X1[0][:, :, :], x1g[0]).then_inc(S["x1_loaded"], 16)

        def group(g, b, more):
            real = not (isinstance(g, int) and g == 0)
            if more:
                await_(sp, S["x2T_loaded"], (g + 1) * 16)
                if real:
                    await_(sp, S["bn_rows"], g)
                    await_(sp, S["expert_copied"], g * BLK)
                sp.dma_start(X2T[1 - b][:, :], x2Tg[g + 1]).then_inc(S["x2T_loaded"], 16)
            if real:
                store(g - 1, 1 - b)
            if more:
                await_(sp, S["x1_loaded"], (g + 1) * 16)
                sp.dma_start(X1[1 - b][:, :, :], x1g[g + 1]).then_inc(S["x1_loaded"], 16)

        def store(g, b):
            await_(sp, S["out_copied"], (g + 1) * GT)
            sp.dma_start(outg[g], OUT[b][:, :, :]).then_inc(S["out_stored"], 16)
            await_(sp, S["out_stored"], (g + 1) * 16)

        steps(sp, group)
        store(GROUPS - 1, 1)

    def pair_sums(eng, j, h, q):
        sx = SIM[q][:, 0, h, :].unsqueeze(2).broadcast_to([P, NK, NK])
        sy = SIM[q][:, 1, h, :].unsqueeze(1).broadcast_to([P, NK, NK])
        return eng.tensor_tensor(SUM[(q * FH + h) % RING][:, :].rearrange("p (i j) -> p i j", i=NK), sx, sy, ALU.add)

    def sum_buffer_free(eng, j, h):
        wait_pos(eng, S["weights_masked"], j * FH + h - RING + 1)

    @block.gpsimd
    def _(pool):
        nc.gpsimd.memset(hb[:, :], -0.5).then_inc(S["half_set"], 1)
        pool.wait_ge(S["half_set"], 1)
        pool.wait_ge(S["bn_variance"], 1)
        nc.gpsimd.tensor_tensor(rb[:, :], vb[:, :], hb[:, :], ALU.pow).then_inc(S["bn_rstd"], 1)

        def group(g, b, more):
            for k in range(GT):
                j = g * GT + k
                pool.wait_ge(S["sim_copied"], j + 1)
                for h in range(FH):
                    sum_buffer_free(pool, j, h)
                    pair_sums(nc.gpsimd, j, h, k).then_inc(S["pair_sums"], 1)

        steps(pool, group)

    @block.scalar
    def _(act):
        def sim_copy(j, q):
            act.wait_ge(S["sim_product"], j + 1)
            nc.scalar.copy(SIM[q][:, :, :, :].rearrange("p a h k -> p (a h k)"), MB[:, :]).then_inc(S["sim_copied"], 1)

        def gelus(g, b, half):
            act.wait_ge(S["expert_copied"], g * BLK + (half + 1) * 4)
            o = GE[b][:, 4 * half:4 * half + 4, :].rearrange("p e n -> p (e n)")
            nc.scalar.activation(o, o, ACT.Gelu).then_inc(S["gelu_ready"], 1)
            nc.scalar.preload_act_table_set("natural_log_exp_and_others")

        def o_copy(g, b, e):
            act.wait_ge(S["expert_product"], g * BLK + e + 1)
            nc.scalar.copy(GE[b][:, e, :], MB[:, :]).then_inc(S["expert_copied"], 1)

        def bnt(g, b):
            act.wait_ge(S["x2T_loaded"], (g + 1) * 16)
            nc.scalar.activation(BNT[b][:, :], X2T[b][:, :], ACT.Identity, scale=ab[:, 0:1], bias=ab[:, 1:2]).then_inc(S["bn_rows"], 1)

        def finish(j, g, b, k):
            act.wait_ge(S["out_product"], j + 1)
            wait_pos(act, S["out_stored"], (g - 1) * 16)
            nc.scalar.copy(OUT[b][:, k, :], POUT[:, :]).then_inc(S["out_copied"], 1)

        nc.scalar.preload_act_table_set("gelu_and_others")
        for e in range(BLK):
            if e == SIM0:
                sim_copy(0, 0)
            act.wait_ge(S["expert_product"], e + 1)
            nc.scalar.activation(GE[0][:, e, :], E[e // 2 % 2][:, e % 2 * GN:(e % 2 + 1) * GN], ACT.Gelu).then_inc(S["expert_copied"], 1)
        act.wait_ge(S["expert_copied"], BLK)
        act.sem_inc(S["gelu_ready"], 2)
        nc.scalar.preload_act_table_set("natural_log_exp_and_others")
        sim_copy(1, 1)

        def small_exp(j):
            act.wait_ge(S["top_less_max"], j + 1)
            nc.scalar.activation(E8[:, :, :].rearrange("p h k -> p (h k)"), D8[:, :, :].rearrange("p h k -> p (h k)"), ACT.Exp).then_inc(S["top_exp"], 1)

        def small_ln(j):
            act.wait_ge(S["exp_sum"], j + 1)
            nc.scalar.activation(LZ[:, :], Z[:, :], ACT.Ln).then_inc(S["log_sum"], 1)

        small_exp(0)
        small_ln(0)

        def group(g, b, more):
            for k in range(GT):
                j = g * GT + k
                q = k % 2
                nxt = more or k < GT - 1
                for h in range(FH):
                    if h == 0:
                        act.wait_ge(S["bias_ready"], j + 1)
                    if h == 5 and k == 1 and more:
                        bnt(g + 1, 1 - b)
                    if h == 1 and not (isinstance(j, int) and j < 2):
                        finish(j - 2, *((g, b, k - 2) if k >= 2 else (g - 1, 1 - b, k + 2)))
                    if h == SSLOT + LEAD and (more or k < 2):
                        wait_pos(act, S["pair_sums"], (j - 1) * FH)
                        sim_copy(j + 2, (k + 2) % 4)
                    then = divmod(k * FH + h - LEAD, FH)
                    if then in OSLOT and more:
                        if then == OSLOT[0]:
                            wait_pos(act, S["experts_weighted"], g * GT)
                        o_copy(g + 1, 1 - b, OSLOT.index(then))
                    act.wait_ge(S["pair_sums"], j * FH + h + 1)
                    wait_pos(act, S["weights_masked"], j * FH + h - 1)
                    nc.scalar.activation(E[h % 2][:, :], SUM[(k * FH + h) % RING][:, :], ACT.Exp, bias=NB[q][:, h:h + 1]).then_inc(S["exp_ready"], 1)
                    if h == 4 and nxt:
                        small_exp(j + 1)
                    if h == 6 and nxt:
                        small_ln(j + 1)
                    if (k, h) in GSLOT and more:
                        gelus(g + 1, 1 - b, GSLOT.index((k, h)))

        steps(act, group)
        for k in (GT - 2, GT - 1):
            finish((GROUPS - 1) * GT + k, GROUPS - 1, 1, k)

    @block.vector
    def _(dve):
        nc.vector.bn_aggr(mvb[:, :], bnst[:, :, :].rearrange("p s n -> p (s n)")).then_inc(S["bn_mean"], 1)
        dve.wait_ge(S["bn_mean"], 1)
        nc.vector.tensor_scalar(vb[:, :], mvb[:, 1:2], EPS, None, ALU.add).then_inc(S["bn_variance"], 1)
        dve.wait_ge(S["bn_rstd"], 1)
        nc.vector.tensor_tensor(ab[:, 0:1], rb[:, :], gb[:, 0:1], ALU.mult).then_inc(S["bn_coef"], 1)
        dve.wait_ge(S["bn_coef"], 1)
        nc.vector.tensor_tensor(mvb[:, 1:2], mvb[:, 0:1], ab[:, 0:1], ALU.mult).then_inc(S["bn_coef"], 1)
        dve.wait_ge(S["bn_coef"], 2)
        nc.vector.tensor_tensor(ab[:, 1:2], gb[:, 1:2], mvb[:, 1:2], ALU.subtract).then_inc(S["bn_coef"], 1)
        dve.wait_ge(S["bn_coef"], 3)

        def choose(part, j, r, q):
            if part == 0:
                await_(dve, S["sim_copied"], j + 1)
            if part < 4:
                for e in range(4 * part, 4 * part + 4):
                    o = nc.vector.max(M8[q][:, e // FH, e % FH, :], SIM[r][:, e // FH, e % FH, :])
                if part == 3:
                    o.then_inc(S["ranked"], 1)
            if part == 4:
                dve.wait_ge(S["ranked"], j + 1)
                x, y = M8[q][:, 0, :, :], M8[q][:, 1, :, :]
                nc.vector.tensor_tensor(CD[:, :, 0:8], x[:, :, 0:1].broadcast_to([P, FH, 8]), y[:, :, :], ALU.add)
                nc.vector.tensor_tensor(CD[:, :, 8:12], x[:, :, 1:2].broadcast_to([P, FH, 4]), y[:, :, 0:4], ALU.add)
                nc.vector.tensor_tensor(CD[:, :, 12:16].rearrange("p h (a b) -> p h a b", a=2),
                                        x[:, :, 2:4].unsqueeze(3).broadcast_to([P, FH, 2, 2]),
                                        y[:, :, 0:2].unsqueeze(2).broadcast_to([P, FH, 2, 2]), ALU.add)
                nc.vector.tensor_tensor(CD[:, :, 16:20], x[:, :, 4:8], y[:, :, 0:1].broadcast_to([P, FH, 4]), ALU.add).then_inc(S["candidates"], 1)
            if part == 5:
                await_(dve, S["candidates"], j + 1)
                for h in range(FH):
                    o = nc.vector.max(TOP[q][:, h, :], CD[:, h, :])
                o.then_inc(S["top_ready"], 1)
                dve.wait_ge(S["top_ready"], j + 1)
                nc.vector.tensor_tensor(D8[:, :, :], TOP[q][:, :, :], TOP[q][:, :, 0:1].broadcast_to([P, FH, TOPK]), ALU.subtract).then_inc(S["top_less_max"], 1)
            if part == 6:
                dve.wait_ge(S["top_exp"], j + 1)
                nc.vector.tensor_reduce(Z[:, :], E8[:, :, :], AX.X, ALU.add).then_inc(S["exp_sum"], 1)
            if part == 7:
                dve.wait_ge(S["log_sum"], j + 1)
                nc.vector.scalar_tensor_tensor(out=NB[q][:, :], in0=LZ[:, :], scalar=-1.0, in1=TOP[q][:, :, 0], op0=ALU.mult, op1=ALU.subtract).then_inc(S["bias_ready"], 1)

        dve.wait_ge(S["x2T_loaded"], 16)
        nc.vector.tensor_scalar(BNT[0][:, :], X2T[0][:, :], ab[:, 0:1], ab[:, 1:2], ALU.mult, ALU.add).then_inc(S["bn_rows"], 1)
        for part in range(8):
            choose(part, 0, 0, 0)

        def experts(j, g, b, k):
            dve.wait_ge(S["weights_turned"], (j + 1) * FH)
            dve.wait_ge(S["gelu_ready"], (g + 1) * 2)
            wait_pos(dve, S["out_product"], j - 1)
            nc.vector.tensor_tensor(CT[k % 2][:, :, :], WT[:, :, :], GE[b][:, :, k * P:(k + 1) * P], ALU.mult).then_inc(S["experts_weighted"], 1)

        def group(g, b, more):
            for k in range(GT):
                j = g * GT + k
                q = k % 2
                prev = (j - 1, g, b, k - 1) if k else (j - 1, g - 1, 1 - b, GT - 1)
                real = not (isinstance(j, int) and j == 0)
                for h in range(FH):
                    if more or k < GT - 1:
                        for part in PARTS[h]:
                            choose(part, j + 1, (k + 1) % 4, 1 - q)
                    if h == 1 and real:
                        experts(*prev)
                    dve.wait_ge(S["exp_ready"], j * FH + h + 1)
                    wait_pos(dve, S["weights_turned"], j * FH + h - WRING + 1)
                    nc.vector.scalar_tensor_tensor(out=W[h % WRING][:, :], in0=SUM[(k * FH + h) % RING][:, :], scalar=TOP[q][:, h, TOPK - 1:TOPK],
                                                   in1=E[h % 2][:, :], op0=ALU.is_ge, op1=ALU.mult).then_inc(S["weights_masked"], 1)

        steps(dve, group)
        experts(GROUPS * GT - 1, GROUPS - 1, 1, GT - 1)

    @block.tensor
    def _(pe):
        def similar(j, g, b, k, o_done):
            pe.wait_ge(S["bn_rows"], g + 1)
            wait_pos(pe, S["sim_copied"], j)
            wait_pos(pe, S["expert_copied"], o_done)
            pe.matmul(MB[:, :], BNT[b][:, k * P:(k + 1) * P], KM[:, :], start=True, stop=True).then_inc(S["sim_product"], 1)

        def blocks_made(g, k, more):
            return (g + 1) * BLK + (sum(1 for at in OSLOT if at < (k, SSLOT)) if more else 0)

        def o_block(g, b, e, sim_done):
            pe.wait_ge(S["x2T_loaded"], (g + 1) * 16)
            wait_pos(pe, S["expert_copied"], g * BLK + e)
            wait_pos(pe, S["sim_copied"], sim_done)
            pe.matmul(MB[:, :], key_in[:, e * P:(e + 1) * P], X2T[b][:, :], start=True, stop=True).then_inc(S["expert_product"], 1)

        for e in range(BLK):
            if e == SIM0:
                similar(0, 0, 0, 0, 0)
            pe.wait_ge(S["x2T_loaded"], 16)
            if e >= 4:
                pe.wait_ge(S["expert_copied"], e - 3)
            pe.matmul(E[e // 2 % 2][:, e % 2 * GN:(e % 2 + 1) * GN], key_in[:, e * P:(e + 1) * P], X2T[0][:, :],
                      start=True, stop=True).then_inc(S["expert_product"], 1)
        similar(1, 0, 0, 1, 0)

        def outputs(j, g, b, k):
            po = POUT[:, :]
            pe.wait_ge(S["x1_loaded"], (g + 1) * 16)
            wait_pos(pe, S["out_copied"], j)
            pe.matmul(po, ident[:, :], X1[b][:, k, :], start=True, stop=False)
            pe.wait_ge(S["experts_weighted"], j + 1)
            for e in range(BLK):
                o = pe.matmul(po, CT[k % 2][:, e, :], key_out[:, e, :], start=False, stop=(e == BLK - 1))
            o.then_inc(S["out_product"], 1)

        def group(g, b, more):
            for k in range(GT):
                j = g * GT + k
                real = not (isinstance(j, int) and j == 0)
                for h in range(FH):
                    if h == SSLOT and (more or k < 2):
                        if k < 2:
                            similar(j + 2, g, b, k + 2, blocks_made(g, k, more))
                        else:
                            similar(j + 2, g + 1, 1 - b, k - 2, blocks_made(g, k, more))
                    if (k, h) in OSLOT and more:
                        o_block(g + 1, 1 - b, OSLOT.index((k, h)), j + 2 + (h >= SSLOT))
                    if h == 3 and real:
                        outputs(j - 1, *((g, b, k - 1) if k else (g - 1, 1 - b, GT - 1)))
                    pe.wait_ge(S["weights_masked"], j * FH + h + 1)
                    if h == 0:
                        wait_pos(pe, S["experts_weighted"], j)
                    for e in range(BLK):
                        o = pe.matmul(WT[:, e, :], W[h % WRING][:, e * P:(e + 1) * P], ident[:, :], is_transpose=True,
                                      start=(h == 0 and e % 4 == 0), stop=(h == FH - 1), skip_group_check=True)
                    o.then_inc(S["weights_turned"], 1)

        steps(pe, group)
        outputs(GROUPS * GT - 1, GROUPS - 1, 1, GT - 1)


def program(nc, x, w_qkvT, w_projT, ident, identb, band, w_q, keysT, key_inT, key_out, gb, out):
    x1 = nc.dram_tensor("x1", (SEQS * T, P), F32, kind="Internal").ap()
    x2T = nc.dram_tensor("x2T", (P, SEQS * T), F32, kind="Internal").ap()
    with ExitStack() as both:
        def sb(name, shape):
            return both.enter_context(nc.sbuf_tensor(name, shape, F32))

        idf = sb("idf", [P, P])
        KI = sb("KI", [P, NE])
        KO = sb("KO", [P, BLK, P])
        KM = sb("KM", [P, 2 * FH * NK])
        GB = sb("GB", [P, 2])
        bnst = sb("bnst", [P, SEQS, 6])
        extra = [(idf[:, :], ident), (KI[:, :], key_inT), (KO[:, :, :], key_out), (GB[:, :], gb)]
        with ExitStack() as ctx:
            attention(nc, ctx, x, w_qkvT, w_projT, identb, band, w_q, keysT, idf, bnst, KM, extra, x1, x2T)
        with ExitStack() as ctx:
            ffn(nc, ctx, x1, x2T, KM, KI, KO, GB, idf, bnst, out)


def kernel(L0_attn_x, L0_attn_w_qkv, L0_attn_w_proj, L0_ffn_gamma, L0_ffn_beta, L0_ffn_w_q, L0_ffn_keys,
           L0_ffn_key_in, L0_ffn_key_out):
    import ml_dtypes
    import numpy as np
    import concourse.bacc as bacc
    from concourse.bass_utils import run_bass_kernel_spmd

    w = np.asarray(L0_attn_w_qkv).reshape(3, P, P)
    dh = [w[n].reshape(H, DK, P).transpose(1, 0, 2).reshape(P, P) for n in range(2)]
    keep = np.arange(P)[None, :] >= np.arange(P)[:, None]
    arrays = {
        "x": np.asarray(L0_attn_x).reshape(SEQS * T, P),
        "w_qkvT": np.concatenate([dh[0].T, dh[1].T, w[2].T], axis=1),
        "w_projT": np.asarray(L0_attn_w_proj).T,
        "ident": np.eye(P, dtype=np.float32),
        "identb": np.eye(P, dtype=np.float32).astype(ml_dtypes.bfloat16),
        "band": np.concatenate([np.where(keep.T, 0, -1e30), np.where(keep, 0, -1e30)], axis=1).astype(ml_dtypes.bfloat16),
        "w_q": np.asarray(L0_ffn_w_q),
        "keysT": np.asarray(L0_ffn_keys).transpose(3, 2, 0, 1).reshape(P, 2 * FH * NK),
        "key_inT": np.asarray(L0_ffn_key_in).T,
        "key_out": np.asarray(L0_ffn_key_out).reshape(BLK, P, P).transpose(1, 0, 2),
        "gb": np.stack([np.asarray(L0_ffn_gamma), np.asarray(L0_ffn_beta)], axis=1),
    }
    arrays = {name: np.ascontiguousarray(a) for name, a in arrays.items()}
    nc = bacc.Bacc("TRN2", target_bir_lowering=False, num_devices=1)
    args = {name: nc.dram_tensor("in_" + name, a.shape, mybir.dt.from_np(a.dtype), kind="ExternalInput").ap()
            for name, a in arrays.items()}
    out = nc.dram_tensor("out_0", (SEQS * T, P), F32, kind="ExternalOutput").ap()
    program(nc, out=out, **args)
    ran = run_bass_kernel_spmd(nc, [{"in_" + name: a for name, a in arrays.items()}], core_ids=[0])
    return ran.results[0]["out_0"].reshape(SEQS, T, P)
```
